# Optimizing a Trainium2 kernel written in Bass

```python
import numpy as np
import jax
import jax.numpy as jnp

def _softmax(x, axis=-1):
    return jax.nn.softmax(x, axis=axis)

def _gelu(x):
    return jax.nn.gelu(x, approximate=True)

def _silu(x):
    return jax.nn.silu(x)

def _sigmoid(x):
    return jax.nn.sigmoid(x)

def _layernorm(x, axis=-1, eps=1e-05):
    m = jnp.mean(x, axis=axis, keepdims=True)
    v = jnp.var(x, axis=axis, keepdims=True)
    return (x - m) / jnp.sqrt(v + eps)

def _scatter_add(tgt, idx, src, axis=0):
    return tgt.at[idx].add(src)

def _segment_sum(src, seg, n):
    return jax.ops.segment_sum(src, seg, n)
kernel_name = 'mk_adj_resnorm_d4_adj_r2_0e10b4'

def setup_inputs(seed: int=0):
    np.random.seed(seed)
    _w = jnp.asarray

    def _rec_inputs():
        import jax
        import jax.numpy as jnp
        _gk = jax.random.key(seed)
        x = -0.000929 + 1 * jax.random.normal(jax.random.fold_in(_gk, 1), (32, 256, 256), jnp.float32)
        _w = (1.0 + jnp.arange(256, dtype=jnp.float32)) ** (-0.5)
        _w = _w / _w.mean()
        _pij = jnp.clip(0.0625 * _w[:, None] * _w[None, :], 0.0, 1.0)
        _a = jax.random.uniform(jax.random.fold_in(_gk, 2), (256, 256)) < _pij
        adj = _a.astype(jnp.int32)
        return (x, adj)
    x, adj = _rec_inputs()

    def _L0_gnn_setup():
        import jax, jax.numpy as jnp
        import numpy as np
        B, K, DIN, DOUT = (32, 64, 256, 256)
        key = jax.random.key(seed)
        k1, k2, k3, k4 = jax.random.split(key, 4)
        x = jax.random.normal(k1, (B, K, DIN), dtype=jnp.float32)
        adj = jax.random.randint(k2, (K, K), 0, 2, dtype=jnp.int32)
        W = jax.random.normal(k3, (DOUT, 2 * DIN), dtype=jnp.float32) * 0.02
        b = jax.random.normal(k4, (DOUT,), dtype=jnp.float32) * 0.02
        return {'x': x, 'adj': adj, 'W': W, 'b': b}
    _L0_gnn_all = _L0_gnn_setup()
    _L0_gnn_in = {k: v for k, v in _L0_gnn_all.items() if k in ('W', 'b')}
    del _L0_gnn_all

    def _L1_gnn_setup():
        import jax, jax.numpy as jnp
        import numpy as np
        D_MODEL = 256
        NUM_HEADS = 8
        D_HEAD = D_MODEL // NUM_HEADS
        B, N = (4, 1024)
        key = jax.random.key(seed)
        ks = jax.random.split(key, 10)
        s = 1.0 / np.sqrt(D_MODEL)
        inp = {'h': jax.random.normal(ks[0], (B, N, D_MODEL), dtype=jnp.float32), 'adj': jax.random.randint(ks[1], (N, N), 0, 2, dtype=jnp.int32), 'Wq': jax.random.uniform(ks[2], (D_MODEL, D_MODEL), jnp.float32, -s, s), 'bq': jax.random.uniform(ks[3], (D_MODEL,), jnp.float32, -s, s), 'Wk': jax.random.uniform(ks[4], (D_MODEL, D_MODEL), jnp.float32, -s, s), 'bk': jax.random.uniform(ks[5], (D_MODEL,), jnp.float32, -s, s), 'Wv': jax.random.uniform(ks[6], (D_MODEL, D_MODEL), jnp.float32, -s, s), 'bv': jax.random.uniform(ks[7], (D_MODEL,), jnp.float32, -s, s), 'Wo': jax.random.uniform(ks[8], (D_MODEL, D_MODEL), jnp.float32, -s, s), 'bo': jax.random.uniform(ks[9], (D_MODEL,), jnp.float32, -s, s)}
        return inp
    _L1_gnn_all = _L1_gnn_setup()
    _L1_gnn_in = {k: v for k, v in _L1_gnn_all.items() if k in ('Wq', 'bq', 'Wk', 'bk', 'Wv', 'bv', 'Wo', 'bo')}
    del _L1_gnn_all

    def _L2_gnn_setup():
        import jax, jax.numpy as jnp
        import numpy as np
        B, N, D = (8, 1024, 256)
        NEG_SLOPE = 0.2
        key = jax.random.key(seed)
        k1, k2, k3, k4, k5 = jax.random.split(key, 5)
        x = jax.random.normal(k1, (B, N, D), dtype=jnp.float32)
        adj = jax.random.randint(k2, (N, N), 0, 2, dtype=jnp.int32)
        adj = jnp.maximum(adj, jnp.eye(N, dtype=jnp.int32))
        W = jax.random.normal(k3, (D, D), dtype=jnp.float32) * (1.0 / np.sqrt(D))
        a_src = jax.random.normal(k4, (D,), dtype=jnp.float32) * (1.0 / np.sqrt(D))
        a_dst = jax.random.normal(k5, (D,), dtype=jnp.float32) * (1.0 / np.sqrt(D))
        return {'x': x, 'adj': adj, 'W': W, 'a_src': a_src, 'a_dst': a_dst}
    _L2_gnn_all = _L2_gnn_setup()
    _L2_gnn_in = {k: v for k, v in _L2_gnn_all.items() if k in ('W', 'a_src', 'a_dst')}
    del _L2_gnn_all

    def _L3_gnn_setup():
        import jax, jax.numpy as jnp
        import numpy as np
        D_MODEL = 256
        NUM_HEADS = 8
        D_HEAD = D_MODEL // NUM_HEADS
        B, N = (4, 1024)
        key = jax.random.key(seed)
        ks = jax.random.split(key, 10)
        s = 1.0 / np.sqrt(D_MODEL)
        inp = {'h': jax.random.normal(ks[0], (B, N, D_MODEL), dtype=jnp.float32), 'adj': jax.random.randint(ks[1], (N, N), 0, 2, dtype=jnp.int32), 'Wq': jax.random.uniform(ks[2], (D_MODEL, D_MODEL), jnp.float32, -s, s), 'bq': jax.random.uniform(ks[3], (D_MODEL,), jnp.float32, -s, s), 'Wk': jax.random.uniform(ks[4], (D_MODEL, D_MODEL), jnp.float32, -s, s), 'bk': jax.random.uniform(ks[5], (D_MODEL,), jnp.float32, -s, s), 'Wv': jax.random.uniform(ks[6], (D_MODEL, D_MODEL), jnp.float32, -s, s), 'bv': jax.random.uniform(ks[7], (D_MODEL,), jnp.float32, -s, s), 'Wo': jax.random.uniform(ks[8], (D_MODEL, D_MODEL), jnp.float32, -s, s), 'bo': jax.random.uniform(ks[9], (D_MODEL,), jnp.float32, -s, s)}
        return inp
    _L3_gnn_all = _L3_gnn_setup()
    _L3_gnn_in = {k: v for k, v in _L3_gnn_all.items() if k in ('Wq', 'bq', 'Wk', 'bk', 'Wv', 'bv', 'Wo', 'bo')}
    del _L3_gnn_all
    return {'x': x, 'adj': adj, 'L0_gnn_W': _L0_gnn_in['W'], 'L0_gnn_b': _L0_gnn_in['b'], 'L1_gnn_Wq': _L1_gnn_in['Wq'], 'L1_gnn_bq': _L1_gnn_in['bq'], 'L1_gnn_Wk': _L1_gnn_in['Wk'], 'L1_gnn_bk': _L1_gnn_in['bk'], 'L1_gnn_Wv': _L1_gnn_in['Wv'], 'L1_gnn_bv': _L1_gnn_in['bv'], 'L1_gnn_Wo': _L1_gnn_in['Wo'], 'L1_gnn_bo': _L1_gnn_in['bo'], 'L2_gnn_W': _L2_gnn_in['W'], 'L2_gnn_a_src': _L2_gnn_in['a_src'], 'L2_gnn_a_dst': _L2_gnn_in['a_dst'], 'L3_gnn_Wq': _L3_gnn_in['Wq'], 'L3_gnn_bq': _L3_gnn_in['bq'], 'L3_gnn_Wk': _L3_gnn_in['Wk'], 'L3_gnn_bk': _L3_gnn_in['bk'], 'L3_gnn_Wv': _L3_gnn_in['Wv'], 'L3_gnn_bv': _L3_gnn_in['bv'], 'L3_gnn_Wo': _L3_gnn_in['Wo'], 'L3_gnn_bo': _L3_gnn_in['bo']}

def reference(x, adj, L0_gnn_W, L0_gnn_b, L1_gnn_Wq, L1_gnn_bq, L1_gnn_Wk, L1_gnn_bk, L1_gnn_Wv, L1_gnn_bv, L1_gnn_Wo, L1_gnn_bo, L2_gnn_W, L2_gnn_a_src, L2_gnn_a_dst, L3_gnn_Wq, L3_gnn_bq, L3_gnn_Wk, L3_gnn_bk, L3_gnn_Wv, L3_gnn_bv, L3_gnn_Wo, L3_gnn_bo):
    import jax
    import jax.numpy as jnp

    def _L0_gnn_ref(x, adj, W, b):
        import jax, jax.numpy as jnp
        import numpy as np
        B, K, DIN, DOUT = (32, 64, 256, 256)
        Din = x.shape[-1]
        Wi, Wj = (W[:, :Din], W[:, Din:])
        mi = jnp.einsum('bkd,od->bko', x, Wi)
        mj = jnp.einsum('bkd,od->bko', x, Wj)
        a = adj.astype(x.dtype)
        deg = a.sum(axis=1)
        out = deg[None, :, None] * (mi + b) + jnp.einsum('ij,bjo->bio', a, mj)
        return out

    def _L1_gnn_ref(h, adj, Wq, bq, Wk, bk, Wv, bv, Wo, bo):
        import jax, jax.numpy as jnp
        import numpy as np
        D_MODEL = 256
        NUM_HEADS = 8
        D_HEAD = D_MODEL // NUM_HEADS
        B, N = (4, 1024)
        b, n, _ = h.shape

        def split_heads(x):
            return x.reshape(b, n, NUM_HEADS, D_HEAD).transpose(0, 2, 1, 3)
        q = split_heads(h @ Wq.T + bq)
        k = split_heads(h @ Wk.T + bk)
        v = split_heads(h @ Wv.T + bv)
        scale = 1.0 / np.sqrt(D_HEAD)
        scores = jnp.einsum('bhqd,bhkd->bhqk', q, k) * scale
        mask = (adj == 0)[None, None, :, :]
        scores = jnp.where(mask, -jnp.inf, scores)
        attn = jax.nn.softmax(scores, axis=-1)
        out = jnp.einsum('bhqk,bhkd->bhqd', attn, v)
        out = out.transpose(0, 2, 1, 3).reshape(b, n, D_MODEL)
        return out @ Wo.T + bo

    def _L2_gnn_ref(x, adj, W, a_src, a_dst):
        import jax, jax.numpy as jnp
        import numpy as np
        B, N, D = (8, 1024, 256)
        NEG_SLOPE = 0.2
        Wh = jnp.einsum('bnd,de->bne', x, W)
        e_src = jnp.einsum('bnd,d->bn', Wh, a_src)
        e_dst = jnp.einsum('bnd,d->bn', Wh, a_dst)
        logits = e_src[:, :, None] + e_dst[:, None, :]
        logits = jnp.where(logits >= 0, logits, NEG_SLOPE * logits)
        mask = (adj == 0)[None, :, :]
        logits = jnp.where(mask, -jnp.inf, logits)
        attn = jax.nn.softmax(logits, axis=-1)
        attn = jnp.nan_to_num(attn, nan=0.0)
        out = jnp.einsum('bnm,bmd->bnd', attn, Wh)
        return out

    def _L3_gnn_ref(h, adj, Wq, bq, Wk, bk, Wv, bv, Wo, bo):
        import jax, jax.numpy as jnp
        import numpy as np
        D_MODEL = 256
        NUM_HEADS = 8
        D_HEAD = D_MODEL // NUM_HEADS
        B, N = (4, 1024)
        b, n, _ = h.shape

        def split_heads(x):
            return x.reshape(b, n, NUM_HEADS, D_HEAD).transpose(0, 2, 1, 3)
        q = split_heads(h @ Wq.T + bq)
        k = split_heads(h @ Wk.T + bk)
        v = split_heads(h @ Wv.T + bv)
        scale = 1.0 / np.sqrt(D_HEAD)
        scores = jnp.einsum('bhqd,bhkd->bhqk', q, k) * scale
        mask = (adj == 0)[None, None, :, :]
        scores = jnp.where(mask, -jnp.inf, scores)
        attn = jax.nn.softmax(scores, axis=-1)
        out = jnp.einsum('bhqk,bhkd->bhqd', attn, v)
        out = out.transpose(0, 2, 1, 3).reshape(b, n, D_MODEL)
        return out @ Wo.T + bo
    x = _layernorm(x + _L0_gnn_ref(x, adj, L0_gnn_W, L0_gnn_b), axis=-1)
    x = _layernorm(x + _L1_gnn_ref(x, adj, L1_gnn_Wq, L1_gnn_bq, L1_gnn_Wk, L1_gnn_bk, L1_gnn_Wv, L1_gnn_bv, L1_gnn_Wo, L1_gnn_bo), axis=-1)
    x = _layernorm(x + _L2_gnn_ref(x, adj, L2_gnn_W, L2_gnn_a_src, L2_gnn_a_dst), axis=-1)
    x = _layernorm(x + _L3_gnn_ref(x, adj, L3_gnn_Wq, L3_gnn_bq, L3_gnn_Wk, L3_gnn_bk, L3_gnn_Wv, L3_gnn_bv, L3_gnn_Wo, L3_gnn_bo), axis=-1)
    return x

_drawn_inputs = setup_inputs


def setup_inputs(seed=0):
    import zlib

    import numpy as np

    out = dict(_drawn_inputs(seed))
    spreads = {}
    factors = {'L1_gnn_bq': 28.193,
     'L1_gnn_bk': 64.0,
     'L3_gnn_bq': 30.588,
     'L3_gnn_bk': 64.0,
     'L3_gnn_bv': 2.875}
    for name, (base, spread) in spreads.items():
        noise = np.random.default_rng([zlib.crc32(name.encode()), seed]).standard_normal(out[name].shape)
        drawn = base * np.exp(spread * noise) if base else spread * noise
        out[name] = jnp.asarray(drawn.astype(out[name].dtype))
    for name, factor in factors.items():
        out[name] = (out[name] * factor).astype(out[name].dtype)
    return out
```

```python
import concourse.bass as bass
from concourse import mybir
from contextlib import ExitStack

F32 = mybir.dt.float32
F32R = mybir.dt.float32r
I32 = mybir.dt.int32
ACT = mybir.ActivationFunctionType
ALU = mybir.AluOpType
AX = mybir.AxisListType

P = 128
B, N, D = 32, 256, 256
NT = N // P
DT = D // P
H = 8
DH = D // H
HG = P // DH
SCALE = DH ** -0.5
EPS = 1e-5
NEG_SLOPE = 0.2
MASKED = -1.0e38
LOWEST = -3.0e38
WE = D + 2
HIGH, LOW = 0, 1


class Graph:

    def __init__(self, t, par):
        self.t, self.par = t, par

    def __add__(self, n):
        k = self.par + n
        return Graph(self.t + k // 2, k % 2)

    def has(self, n):
        return not isinstance(self.t, int) or 0 <= 2 * self.t + self.par + n < B

    def count(self, k=1, c=0):
        return self.t * (2 * k) + (self.par * k + c)

    def turns(self, k=1, c=0):
        return self.t * k + c


def wait(eng, sem, value):
    if not isinstance(value, int) or value > 0:
        eng.wait_ge(sem, value)


def pipeline(eng, step):
    for n in range(-2, 4):
        step(Graph(n // 2, n % 2))
    with eng.Fori(0, (B - 6) // 2) as t:
        step(Graph(t + 2, 0))
        step(Graph(t + 2, 1))
    for n in range(B - 2, B + 2):
        step(Graph(n // 2, n % 2))


def graph_layers_kernel(nc, x, adj, L0_W, L0_b, L1_Wq, L1_bq, L1_Wk, L1_bk, L1_Wv, L1_bv, L1_Wo, L1_bo,
                        L2_W, L2_a_src, L2_a_dst,
                        L3_Wq, L3_bq, L3_Wk, L3_bk, L3_Wv, L3_bv, L3_Wo, L3_bo, out):
    ctx = ExitStack()
    with ctx:
        def sb(name, shape, dt=F32):
            return ctx.enter_context(nc.sbuf_tensor(name, shape, dt))

        def sem(name):
            return ctx.enter_context(nc.semaphore(name))

        x_res = sb("x_res", [P, B, NT * D])
        ident = sb("ident", [P, P])
        mask = sb("mask", [P, NT, N])
        row_any = sb("row_any", [P, NT])
        defined = sb("defined", [P, NT])
        deg = sb("deg", [P, NT])
        w0 = [sb(f"w0_{p}", [P, DT, 2 * D], F32R) for p in "hl"]
        wt = {(L, n): [sb(f"w{L}{n}_{p}", [P, DT, D], F32R) for p in "hl"] for L in (1, 3) for n in "qkvo"}
        w2 = [sb(f"w2_{p}", [P, DT, WE], F32R) for p in "hl"]
        dst_rep = [sb(f"dst_rep_{p}", [P, DT, P], F32R) for p in "hl"]
        bias_q = {L: sb(f"bias_q{L}", [P, DT]) for L in (1, 3)}
        bias_k = {L: sb(f"bias_k{L}", [P, DT]) for L in (1, 3)}
        bias_v = {L: sb(f"bias_v{L}", [P, DT]) for L in (1, 3)}
        bias_o = {L: sb(f"bias_o{L}", [P, D]) for L in (1, 3)}

        x_in = sb("x_in", [P, 2, NT * D])
        xt = [sb(f"xt_{p}", [P, DT, N], F32R) for p in "hl"]
        xb = sb("xb", [P, 2, NT * D])
        q_parts = sb("q_parts", [P, 2, DT, N], F32R)
        k_parts = [sb(f"k_parts{i}", [P, 2, DT, N], F32R) for i in range(2)]
        qz = [sb(f"qz{i}", [P, HG, 2, DT, N], F32R) for i in range(2)]
        v_sb = sb("v_sb", [P, 2, NT, WE])
        probs = sb("probs", [P, 4, NT, N])
        probs_t = sb("probs_t", [P, 4, NT * N])
        maxes = sb("maxes", [P, 2, 2 * H])
        neg_max = sb("neg_max", [P, 2, 2 * H])
        sums = sb("sums", [P, 2, 2 * H])
        recip = sb("recip", [P, 2 * H])
        recip_rep = sb("recip_rep", [P, NT, D])
        recip_t = sb("recip_t", [P, DT, N])
        o_t = sb("o_t", [P, DT, N])
        o_parts = [sb(f"o_t_{p}", [P, DT, N], F32R) for p in "hl"]
        y_sb = sb("y_sb", [P, NT, D])
        y_out = sb("y_out", [P, 2, NT * D])
        node_max = sb("node_max", [P, 3, NT])
        src_recip = sb("src_recip", [P, 2, NT])
        stats = sb("stats", [P, NT, 6])
        mean_var = sb("mean_var", [P, NT, 2])
        var_eps = sb("var_eps", [P, NT])
        rstd = sb("rstd", [P, NT])
        minus_half = sb("minus_half", [P, NT])

        adj_t = recip_t
        deg_b = o_t

        ps = ctx.enter_context(nc.psum_tensor("ps", [P, 8, 512], F32))
        BANK_X, BANK_O, BANK_PROJ, BANK_S, BANK_PT = 0, 1, 2, 4, 6

        raw_names = ["0i", "0j", "1q", "1k", "1v", "1o", "3q", "3k", "3v", "3o"]
        raw_src = {"0i": L0_W[:, 0:D], "0j": L0_W[:, D:2 * D], "1q": L1_Wq, "1k": L1_Wk, "1v": L1_Wv,
                   "1o": L1_Wo, "3q": L3_Wq, "3k": L3_Wk, "3v": L3_Wv, "3o": L3_Wo}
        raw = {n: x_res[:, i, :].rearrange("p (t d) -> p t d", t=DT) for i, n in enumerate(raw_names)}
        raw2 = x_res[:, 10, :].rearrange("p (t d) -> p t d", t=DT)
        adj_i = x_res[:, 11, :].rearrange("p (t d) -> p t d", t=NT).bitcast(I32)
        adj_f = x_res[:, 20, :].rearrange("p (t n) -> p t n", t=NT)
        rows = {n: x_res[:, 12 + i, 0:D] for i, n in enumerate(["b0", "bo1", "bo3", "asrc", "adst"])}
        zeros = x_res[:, 17, 0:P]
        scratch = x_res[:, 18, 0:D]
        va = x_res[:, 19, 0:4]
        bv_rep = {L: [o_parts[p][:, :, 0:P] if L == 1 else o_parts[p][:, :, P:2 * P] for p in (0, 1)]
                  for L in (1, 3)}
        row_src = {"b0": L0_b, "bo1": L1_bo, "bo3": L3_bo, "asrc": L2_a_src, "adst": L2_a_dst}

        def weight_dst(n, p):
            if n == "0i":
                return w0[p][:, :, 0:D]
            if n == "0j":
                return w0[p][:, :, D:2 * D]
            return wt[(int(n[0]), n[1])][p][:, :, :]

        adj_loaded = sem("adj_loaded")
        weight_loaded = {n: sem(f"weight_loaded_{n}") for n in raw_names + ["2"]}
        rows_loaded = sem("rows_loaded")
        ident_ready = sem("ident_ready")
        consts_ready = sem("consts_ready")
        wt_transposed = sem("wt_transposed")
        wt_high = sem("wt_high")
        wt_low = sem("wt_low")
        prep_step = sem("prep_step")
        bias_product = sem("bias_product")
        qz_zeroed = sem("qz_zeroed")
        prepared = sem("prepared")
        apart = sem("apart")
        layer_done = [[sem(f"layer{L}_stored{p}") for p in range(2)] for L in range(4)]

        def start_of_layer(eng, L):
            if L == 0:
                eng.wait_ge(prepared, 1)
            else:
                eng.wait_ge(layer_done[L - 1][0], 16 * (B // 2))
                eng.wait_ge(layer_done[L - 1][1], 16 * (B // 2))

        def part(eng):
            eng.sem_inc(apart, 1)

        def three_pass(pe_out, pairs):
            n = len(pairs) * 3
            i = 0
            for st, mv in pairs:
                for a, b in ((HIGH, HIGH), (HIGH, LOW), (LOW, HIGH)):
                    last = nc.tensor.matmul(pe_out, st[a], mv[b], start=(i == 0), stop=(i == n - 1))
                    i += 1
            return last

        N_RAW = len(raw_names)

        def prep_sync(sp):
            sp.dma_start(raw["0i"], raw_src["0i"].rearrange("(t p) d -> p t d", p=P)).then_inc(weight_loaded["0i"], 16)
            sp.dma_start(adj_i, adj.rearrange("(t p) d -> p t d", p=P)).then_inc(adj_loaded, 16)
            for n in raw_names[1:]:
                sp.dma_start(raw[n], raw_src[n].rearrange("(t p) d -> p t d", p=P)).then_inc(weight_loaded[n], 16)
            sp.dma_start(raw2, L2_W.rearrange("(t p) d -> p t d", p=P)).then_inc(weight_loaded["2"], 16)
            for n, src in row_src.items():
                sp.dma_start(rows[n], src.partition_broadcast(P)).then_inc(rows_loaded, 16)
            for dst, src in ((bias_q[1], L1_bq), (bias_k[1], L1_bk), (bias_v[1], L1_bv),
                             (bias_q[3], L3_bq), (bias_k[3], L3_bk), (bias_v[3], L3_bv)):
                sp.dma_start(dst[:], src.rearrange("(t p) -> p t", p=P), allow_slow_non_contiguous=True).then_inc(rows_loaded, 16)

        def prep_gpsimd(pool):
            nc.gpsimd.memset(ident[:], 0.0).then_inc(ident_ready, 1)
            pool.wait_ge(ident_ready, 1)
            nc.gpsimd.affine_select(out=ident[:], in_=ident[:], compare_op=ALU.not_equal, fill=1.0, base=0,
                                    pattern=[[-1, P]], channel_multiplier=1).then_inc(ident_ready, 1)
            nc.gpsimd.memset(zeros, 0.0).then_inc(consts_ready, 1)
            nc.gpsimd.memset(minus_half[:], -0.5).then_inc(consts_ready, 1)
            for i in range(2):
                nc.gpsimd.memset(qz[i][:].bitcast(F32).rearrange("p a b c d -> p (a b c d)"), 0.0).then_inc(qz_zeroed, 1)

        def prep_tensor(pe):
            pe.wait_ge(ident_ready, 2)
            for i, n in enumerate(raw_names):
                pe.wait_ge(weight_loaded[n], 16)
                wait(pe, wt_low, i - 3)
                for dt in range(DT):
                    for ot in range(DT):
                        last = nc.tensor.transpose(ps[:, i % 4, dt * D + ot * P:dt * D + (ot + 1) * P],
                                                   raw[n][:, ot, dt * P:(dt + 1) * P], ident[:])
                last.then_inc(wt_transposed, 1)
            pe.wait_ge(prep_step, 1)
            for jt in range(NT):
                for it in range(NT):
                    last = nc.tensor.transpose(ps[:, 4, jt * N + it * P:jt * N + (it + 1) * P],
                                               adj_f[:, it, jt * P:(jt + 1) * P], ident[:])
            last.then_inc(wt_transposed, 1)
            pe.wait_ge(wt_low, N_RAW)
            pe.wait_ge(consts_ready, 4)
            for L in (1, 3):
                last = three_pass(ps[:, 5 + L // 2, 0:D],
                                  [([bv_rep[L][p][:, ct, :] for p in (0, 1)],
                                    [wt[(L, "o")][p][:, ct, :] for p in (0, 1)]) for ct in range(DT)])
            last.then_inc(bias_product, 1)

        def prep_scalar(act):
            for i, n in enumerate(raw_names):
                act.wait_ge(wt_transposed, i + 1)
                nc.scalar.activation(weight_dst(n, HIGH), ps[:, i % 4, :].rearrange("p (t d) -> p t d", t=DT),
                                     ACT.Copy).then_inc(wt_high, 1)

        def prep_vector(dve):
            done = [0]

            def link(ins):
                done[0] += 1
                ins.then_inc(prep_step, 1)
                dve.wait_ge(prep_step, done[0])

            dve.wait_ge(adj_loaded, 16)
            link(nc.vector.tensor_copy(adj_f, adj_i))
            for i, n in enumerate(raw_names):
                dve.wait_ge(wt_high, i + 1)
                nc.vector.tensor_tensor(weight_dst(n, LOW), ps[:, i % 4, :].rearrange("p (t d) -> p t d", t=DT),
                                        weight_dst(n, HIGH).bitcast(F32), ALU.subtract).then_inc(wt_low, 1)
            link(nc.vector.reduce_sum(deg[:], adj_f, AX.X))
            link(nc.vector.tensor_scalar(mask[:], adj_f, 0.0, MASKED, ALU.is_equal, ALU.mult))
            link(nc.vector.reduce_max(row_any[:], mask[:], AX.X))
            link(nc.vector.tensor_scalar(row_any[:], row_any[:], 0.0, None, ALU.is_equal))
            link(nc.vector.reciprocal(defined[:], row_any[:]))
            link(nc.vector.tensor_tensor(defined[:], defined[:], row_any[:], ALU.mult))
            dve.wait_ge(wt_transposed, N_RAW + 1)
            link(nc.vector.tensor_copy(adj_t[:].rearrange("p t n -> p (t n)"), ps[:, 4, :]))
            dve.wait_ge(rows_loaded, 16 * 11)
            for nt in range(NT):
                link(nc.vector.tensor_scalar(deg_b[:, nt, :], rows["b0"], deg[:, nt:nt + 1], None, ALU.mult))
            dve.wait_ge(weight_loaded["2"], 16)
            for i, row in enumerate(("asrc", "adst")):
                for dt in range(DT):
                    link(nc.vector.tensor_tensor_reduce(scratch, raw2[:, dt, :], rows[row], 1.0, 0.0,
                                                        ALU.mult, ALU.add, va[:, 2 * i + dt:2 * i + dt + 1]))
            dve.wait_ge(consts_ready, 2)
            link(nc.vector.tensor_copy(w2[HIGH][:, :, 0:D], raw2))
            link(nc.vector.tensor_tensor(w2[LOW][:, :, 0:D], raw2, w2[HIGH][:, :, 0:D].bitcast(F32), ALU.subtract))

            def split_column(high, low, col, n):
                link(nc.vector.tensor_scalar(high, zeros[:, 0:n], col, None, ALU.add))
                return nc.vector.scalar_tensor_tensor(out=low, in0=zeros[:, 0:n], scalar=col,
                                                      in1=high.bitcast(F32), op0=ALU.add, op1=ALU.subtract)

            for dt in range(DT):
                link(split_column(w2[HIGH][:, dt, D:WE], w2[LOW][:, dt, D:WE], va[:, dt:dt + 1], WE - D))
                link(split_column(dst_rep[HIGH][:, dt, :], dst_rep[LOW][:, dt, :], va[:, 2 + dt:3 + dt], P))
                for L in (1, 3):
                    link(split_column(bv_rep[L][HIGH][:, dt, :], bv_rep[L][LOW][:, dt, :],
                                      bias_v[L][:, dt:dt + 1], P))
            link(nc.vector.tensor_copy(scratch, rows["bo1"]))
            nc.vector.tensor_copy(scratch, rows["bo3"]).then_inc(consts_ready, 2)
            dve.wait_ge(bias_product, 1)
            link(nc.vector.tensor_tensor(bias_o[1][:], ps[:, 5, 0:D], rows["bo1"], ALU.add))
            nc.vector.tensor_tensor(bias_o[3][:], ps[:, 6, 0:D], rows["bo3"], ALU.add).then_inc(prepared, 1)

        class Layer:

            def __init__(self, L, names, loops=()):
                self.L = L
                shared = ["xt_ps", "xt_high", "xt_low", "xb_ready", "y_ps", "y_summed", "y_stats", "y_var",
                          "var_eps_ready", "rstd_ready", "out_ready"]
                self.s = {n: sem(f"L{L}_{n}") for n in shared + names}
                self.x_loaded = [sem(f"L{L}_x_loaded{p}") for p in range(2)]
                self.stored = layer_done[L]

            def load(self, sp, g):
                wait(sp, self.s["xt_ps"], g.count(1, -1))
                wait(sp, self.s["xb_ready"], g.count(1, -1))
                dst = x_in[:, g.par, :]
                if self.L == 0:
                    sp.dma_start(dst.rearrange("p (t d) -> p t d", t=NT),
                                 x.rearrange("b (t p) d -> p (b t) d", p=P)[:, bass.ds(g.count(NT), NT), :]
                                 ).then_inc(self.x_loaded[g.par], 16)
                else:
                    sp.dma_start(dst, x_res[:, bass.ds(g.count(), 1), :].rearrange("p a n -> p (a n)")
                                 ).then_inc(self.x_loaded[g.par], 16)

            def store(self, sp, g):
                sp.wait_ge(self.s["out_ready"], g.count(1, 1))
                src = y_out[:, g.par, :]
                if self.L == 3:
                    sp.dma_start(out.rearrange("b (t p) d -> p (b t) d", p=P)[:, bass.ds(g.count(NT), NT), :],
                                 src.rearrange("p (t d) -> p t d", t=NT)).then_inc(self.stored[g.par], 16)
                else:
                    sp.dma_start(x_res[:, bass.ds(g.count(), 1), :].rearrange("p a n -> p (a n)"), src
                                 ).then_inc(self.stored[g.par], 16)

            def pe_transpose_x(self, pe, g):
                pe.wait_ge(self.x_loaded[g.par], g.turns(16, 16))
                wait(pe, self.s["xt_low"], g.count())
                for dt in range(DT):
                    for nt in range(NT):
                        last = nc.tensor.transpose(
                            ps[:, BANK_X, dt * N + nt * P:dt * N + (nt + 1) * P],
                            x_in[:, g.par, nt * D + dt * P:nt * D + (dt + 1) * P], ident[:])
                last.then_inc(self.s["xt_ps"], 1)

            def act_xt_high(self, act, g, xt_used):
                act.wait_ge(self.s["xt_ps"], g.count(1, 1))
                wait(act, xt_used, g.count())
                nc.scalar.activation(xt[HIGH][:].rearrange("p t n -> p (t n)"), ps[:, BANK_X, :], ACT.Copy
                                     ).then_inc(self.s["xt_high"], 1)

            def dve_xt_low(self, dve, g):
                dve.wait_ge(self.s["xt_high"], g.count(1, 1))
                nc.vector.tensor_tensor(xt[LOW][:].rearrange("p t n -> p (t n)"), ps[:, BANK_X, :],
                                        xt[HIGH][:].bitcast(F32).rearrange("p t n -> p (t n)"),
                                        ALU.subtract).then_inc(self.s["xt_low"], 1)

            def dve_stats(self, dve, g):
                dve.wait_ge(self.s["y_summed"], g.count(1, 1))
                for nt in range(NT):
                    last = nc.vector.bn_stats(stats[:, nt, :], y_sb[:, nt, :])
                last.then_inc(self.s["y_stats"], 1)
                dve.wait_ge(self.s["y_stats"], g.count(1, 1))
                wait(dve, self.s["rstd_ready"], g.count())
                part(dve)
                for nt in range(NT):
                    last = nc.vector.bn_aggr(mean_var[:, nt, :], stats[:, nt, :])
                last.then_inc(self.s["y_var"], 1)

            def pool_rstd(self, pool, g):
                pool.wait_ge(self.s["y_var"], g.count(1, 1))
                part(pool)
                nc.gpsimd.tensor_scalar(var_eps[:], mean_var[:, :, 1], EPS, 1.0, ALU.add, ALU.mult
                                        ).then_inc(self.s["var_eps_ready"], 1)
                pool.wait_ge(self.s["var_eps_ready"], g.count(1, 1))
                wait(pool, self.s["out_ready"], g.count())
                nc.gpsimd.tensor_tensor(rstd[:], var_eps[:], minus_half[:], ALU.pow
                                        ).then_inc(self.s["rstd_ready"], 1)

            def dve_normalize(self, dve, g):
                dve.wait_ge(self.s["rstd_ready"], g.count(1, 1))
                wait(dve, self.stored[g.par], g.turns(16))
                for nt in range(NT):
                    last = nc.vector.tensor_scalar(y_out[:, g.par, nt * D:(nt + 1) * D], y_sb[:, nt, :],
                                                   mean_var[:, nt, 0:1], rstd[:, nt:nt + 1],
                                                   ALU.subtract, ALU.mult)
                last.then_inc(self.s["out_ready"], 1)

            def pool_xb(self, pool, g, const):
                pool.wait_ge(self.x_loaded[g.par], g.turns(16, 16))
                wait(pool, self.s["y_summed"], g.count(1, -1))
                for nt in range(NT):
                    s = slice(nt * D, (nt + 1) * D)
                    if const is None:
                        part(pool)
                        last = nc.gpsimd.tensor_copy(xb[:, g.par, s], x_in[:, g.par, s])
                    else:
                        last = nc.gpsimd.tensor_tensor(xb[:, g.par, s], x_in[:, g.par, s], const[nt], ALU.add)
                last.then_inc(self.s["xb_ready"], 1)

        class MessagePassing(Layer):
            def __init__(self, L):
                super().__init__(L, ["m_ps", "mj_ready", "mi_scaled"])

            def sync(self, sp):
                start_of_layer(sp, self.L)

                def step(g):
                    if g.has(2):
                        self.load(sp, g + 2)
                    if g.has(-2):
                        self.store(sp, g + -2)
                pipeline(sp, step)

            def gpsimd(self, pool):
                start_of_layer(pool, self.L)

                def step(g):
                    if g.has(1):
                        self.pool_xb(pool, g + 1, [deg_b[:, nt, :] for nt in range(NT)])
                    if g.has(-1):
                        self.pool_rstd(pool, g + -1)
                pipeline(pool, step)

            def tensor(self, pe):
                start_of_layer(pe, self.L)
                S = self.s

                def products(g):
                    pe.wait_ge(S["xt_high"], g.count(1, 1))
                    pe.wait_ge(S["xt_low"], g.count(1, 1))
                    wait(pe, S["mi_scaled"], g.count(1, -1))
                    for nt in range(NT):
                        last = three_pass(ps[:, 2 + 2 * g.par + nt, :],
                                          [([xt[p][:, kt, nt * P:(nt + 1) * P] for p in (0, 1)],
                                            [w0[p][:, kt, :] for p in (0, 1)]) for kt in range(DT)])
                    last.then_inc(S["m_ps"], 1)

                def mix(g):
                    pe.wait_ge(S["mj_ready"], g.count(1, 1))
                    wait(pe, S["y_summed"], g.count(1, -1))
                    for it in range(NT):
                        for jt in range(NT):
                            last = nc.tensor.matmul(ps[:, 6 + g.par, it * D:(it + 1) * D],
                                                    adj_t[:, jt, it * P:(it + 1) * P],
                                                    v_sb[:, g.par, jt, 0:D], start=(jt == 0), stop=(jt == NT - 1))
                    last.then_inc(S["y_ps"], 1)

                def step(g):
                    if g.has(1):
                        self.pe_transpose_x(pe, g + 1)
                    if g.has(0):
                        products(g)
                    if g.has(-1):
                        mix(g + -1)
                pipeline(pe, step)

            def scalar(self, act):
                start_of_layer(act, self.L)
                S = self.s

                def step(g):
                    if g.has(0):
                        act.wait_ge(S["m_ps"], g.count(1, 1))
                        wait(act, S["y_ps"], g.count(1, -1))
                        nc.scalar.activation(v_sb[:, g.par, :, 0:D],
                                             ps[:, 2 + 2 * g.par:4 + 2 * g.par, D:2 * D], ACT.Copy
                                             ).then_inc(S["mj_ready"], 1)
                    if g.has(1):
                        self.act_xt_high(act, g + 1, S["m_ps"])
                pipeline(act, step)

            def vector(self, dve):
                start_of_layer(dve, self.L)
                S = self.s

                def scale_mi(g):
                    dve.wait_ge(S["mj_ready"], g.count(1, 1))
                    dve.wait_ge(S["xb_ready"], g.count(1, 1))
                    for nt in range(NT):
                        last = nc.vector.scalar_tensor_tensor(
                            out=probs[:, g.par, nt, :], in0=ps[:, 2 + 2 * g.par + nt, 0:D],
                            scalar=deg[:, nt:nt + 1], in1=xb[:, g.par, nt * D:(nt + 1) * D],
                            op0=ALU.mult, op1=ALU.add)
                    last.then_inc(S["mi_scaled"], 1)

                def y_sum(g):
                    dve.wait_ge(S["y_ps"], g.count(1, 1))
                    dve.wait_ge(S["mi_scaled"], g.count(1, 1))
                    wait(dve, S["out_ready"], g.count())
                    nc.vector.tensor_tensor(y_sb[:].rearrange("p t d -> p (t d)"), ps[:, 6 + g.par, :],
                                            probs[:, g.par, :, :].rearrange("p t d -> p (t d)"), ALU.add
                                            ).then_inc(S["y_summed"], 1)

                def step(g):
                    if g.has(-2):
                        self.dve_normalize(dve, g + -2)
                    if g.has(1):
                        self.dve_xt_low(dve, g + 1)
                    if g.has(0):
                        scale_mi(g)
                    if g.has(-1):
                        y_sum(g + -1)
                        self.dve_stats(dve, g + -1)
                pipeline(dve, step)

        class Attention(Layer):

            def __init__(self, L):
                super().__init__(L, ["q_ps", "k_ps", "v_ps", "q_high", "q_low", "k_high", "k_low", "v_ready",
                                     "scores_ps", "max_ready", "neg_max_ready", "exp_ready",
                                     "pt_ps",
                                     "pt_even", "pt_odd",
                                     "pv_done",
                                     "recip_ready", "recip_rep_ready", "recip_t_ps", "recip_t_ready",
                                     "o_ready", "o_high", "o_low"])
                self.qz_ready = [sem(f"L{L}_qz_ready{p}") for p in range(2)]

            def sync(self, sp):
                start_of_layer(sp, self.L)
                sp.wait_ge(qz_zeroed, 2)
                S = self.s

                def spread_q(g):
                    sp.wait_ge(S["q_low"], g.count(1, 1))
                    part(sp)
                    wait(sp, S["scores_ps"], g.count(H, -H))
                    for a in range(HG):
                        rows_a = slice(a * DH, (a + 1) * DH)
                        sp.dma_start(qz[g.par][rows_a, a].bitcast(F32).rearrange("p a t n -> p (a t n)"),
                                     q_parts[rows_a].bitcast(F32).rearrange("p a t n -> p (a t n)")
                                     ).then_inc(self.qz_ready[g.par], 16)

                def step(g):
                    if g.has(2):
                        self.load(sp, g + 2)
                    if g.has(1):
                        spread_q(g + 1)
                    if g.has(-1):
                        self.store(sp, g + -1)
                pipeline(sp, step)

            def gpsimd(self, pool):
                start_of_layer(pool, self.L)
                S = self.s

                def o_low(g):
                    pool.wait_ge(S["o_high"], g.count(1, 1))
                    nc.gpsimd.tensor_tensor(o_parts[LOW][:].rearrange("p t n -> p (t n)"),
                                            o_t[:].rearrange("p t n -> p (t n)"),
                                            o_parts[HIGH][:].bitcast(F32).rearrange("p t n -> p (t n)"),
                                            ALU.subtract).then_inc(S["o_low"], 1)

                def step(g):
                    if g.has(-1):
                        o_low(g + -1)
                        self.pool_rstd(pool, g + -1)
                    if g.has(1):
                        self.pool_xb(pool, g + 1, [bias_o[self.L][:]] * NT)
                pipeline(pool, step)

            def tensor(self, pe):
                start_of_layer(pe, self.L)
                S = self.s
                W = {n: wt[(self.L, n)] for n in "qkvo"}

                def project_t(w, bank):
                    for ot in range(DT):
                        last = three_pass(ps[:, bank, ot * N:(ot + 1) * N],
                                          [([w[p][:, kt, ot * P:(ot + 1) * P] for p in (0, 1)],
                                            [xt[p][:, kt, :] for p in (0, 1)]) for kt in range(DT)])
                    return last

                def q(g):
                    pe.wait_ge(S["xt_high"], g.count(1, 1))
                    pe.wait_ge(S["xt_low"], g.count(1, 1))
                    wait(pe, S["v_ready"], g.count())
                    project_t(W["q"], BANK_PROJ).then_inc(S["q_ps"], 1)

                def k(g):
                    wait(pe, S["y_summed"], g.count(1, -2))
                    project_t(W["k"], BANK_PROJ + 1).then_inc(S["k_ps"], 1)

                def v(g):
                    pe.wait_ge(S["q_low"], g.count(1, 1))
                    for nt in range(NT):
                        last = three_pass(ps[:, BANK_PROJ, nt * D:(nt + 1) * D],
                                          [([xt[p][:, kt, nt * P:(nt + 1) * P] for p in (0, 1)],
                                            [W["v"][p][:, kt, :] for p in (0, 1)]) for kt in range(DT)])
                    last.then_inc(S["v_ps"], 1)

                def scores(g, h):
                    ot, a = divmod(h, HG)
                    if h == 0:
                        pe.wait_ge(self.qz_ready[g.par], g.turns(16 * HG, 16 * HG))
                        pe.wait_ge(S["k_low"], g.count(1, 1))
                    wait(pe, S["max_ready"], g.count(H, h - 1))
                    for qt in range(NT):
                        last = three_pass(ps[:, BANK_S + h % 2, qt * N:(qt + 1) * N],
                                          [([qz[g.par][:, a, p, ot, qt * P:(qt + 1) * P] for p in (0, 1)],
                                            [k_parts[g.par][:, p, ot, :] for p in (0, 1)])])
                    last.then_inc(S["scores_ps"], 1)

                def transpose_probs(g, h):
                    pe.wait_ge(S["exp_ready"], g.count(H, h + 1))
                    wait(pe, S["pt_odd" if h % 2 else "pt_even"], g.count(H // 2, h // 2))
                    for kt in range(NT):
                        for qt in range(NT):
                            last = nc.tensor.transpose(
                                ps[:, BANK_PT + h % 2, kt * N + qt * P:kt * N + (qt + 1) * P],
                                probs[:, h % 4, qt, kt * P:(kt + 1) * P], ident[:])
                    last.then_inc(S["pt_ps"], 1)

                def pv(g, ot):
                    if ot == 0:
                        pe.wait_ge(S["v_ready"], g.count(1, 1))
                        wait(pe, S["o_ready"], g.count())
                    pe.wait_ge(S["pt_even"], g.count(H // 2, 2 * ot + 2))
                    pe.wait_ge(S["pt_odd"], g.count(H // 2, 2 * ot + 2))
                    for kt in range(NT):
                        for a in range(HG):
                            h = ot * HG + a
                            last = nc.tensor.matmul(ps[a * DH:(a + 1) * DH, BANK_O, ot * N:(ot + 1) * N],
                                                    v_sb[:, g.par, kt, h * DH:(h + 1) * DH],
                                                    probs_t[:, h % 4, kt * N:(kt + 1) * N],
                                                    start=(kt == 0), stop=(kt == NT - 1))
                    last.then_inc(S["pv_done"], 1)

                def transpose_recip(g):
                    pe.wait_ge(S["recip_rep_ready"], g.count(1, 1))
                    wait(pe, S["recip_t_ready"], g.count())
                    if g.has(2):
                        pe.wait_ge(S["xt_low"], g.count(1, 3))
                    for ot in range(DT):
                        for qt in range(NT):
                            last = nc.tensor.transpose(
                                ps[:, BANK_X, ot * N + qt * P:ot * N + (qt + 1) * P],
                                recip_rep[:, qt, ot * P:(ot + 1) * P], ident[:])
                    last.then_inc(S["recip_t_ps"], 1)

                def project_out(g):
                    pe.wait_ge(S["o_high"], g.count(1, 1))
                    pe.wait_ge(S["o_low"], g.count(1, 1))
                    wait(pe, S["y_summed"], g.count())
                    if g.has(2):
                        pe.wait_ge(S["k_low"], g.count(1, 3))
                    for nt in range(NT):
                        last = three_pass(ps[:, BANK_PROJ + 1, nt * D:(nt + 1) * D],
                                          [([o_parts[p][:, ot, nt * P:(nt + 1) * P] for p in (0, 1)],
                                            [W["o"][p][:, ot, :] for p in (0, 1)]) for ot in range(DT)])
                    last.then_inc(S["y_ps"], 1)

                def step(g):
                    now, after, before = g.has(0), g.has(1), g.has(-1)
                    for h in range(H):
                        if h == 0 and after:
                            wait(pe, S["recip_t_ready"], g.count(1, -1))
                            self.pe_transpose_x(pe, g + 1)
                        if now:
                            scores(g, h)
                        if h == 2 and before:
                            pv(g + -1, 1)
                        if h == 6 and now:
                            pv(g, 0)
                        if h < 2 and before:
                            transpose_probs(g + -1, H - 2 + h)
                        if h >= 2 and now:
                            transpose_probs(g, h - 2)
                        if h == 1 and after:
                            q(g + 1)
                        if h == 2 and before:
                            transpose_recip(g + -1)
                        if h == 3 and after:
                            k(g + 1)
                        if h == 4 and after:
                            v(g + 1)
                        if h == 5 and before:
                            project_out(g + -1)
                pipeline(pe, step)

            def scalar(self, act):
                start_of_layer(act, self.L)
                S = self.s

                def biased(dst, bank, bias, done):
                    for ot in range(DT):
                        last = nc.scalar.activation(dst[:, ot, :], ps[:, bank, ot * N:(ot + 1) * N],
                                                    ACT.Identity, bias=bias[:, ot:ot + 1])
                    last.then_inc(done, 1)

                def q_high(g):
                    act.wait_ge(S["q_ps"], g.count(1, 1))
                    p = g + -1
                    wait(act, self.qz_ready[p.par], p.turns(16 * HG, 16 * HG))
                    biased(q_parts[:, HIGH], BANK_PROJ, bias_q[self.L], S["q_high"])

                def k_high(g):
                    act.wait_ge(S["k_ps"], g.count(1, 1))
                    biased(k_parts[g.par][:, HIGH], BANK_PROJ + 1, bias_k[self.L], S["k_high"])

                def v_copy(g):
                    act.wait_ge(S["v_ps"], g.count(1, 1))
                    nc.scalar.activation(v_sb[:, g.par, :, 0:D],
                                         ps[:, BANK_PROJ, :].rearrange("p (t d) -> p t d", t=NT), ACT.Copy
                                         ).then_inc(S["v_ready"], 1)

                def exps(g, h):
                    act.wait_ge(S["neg_max_ready"], g.count(H, h + 1))
                    for qt in range(NT):
                        j = NT * h + qt
                        last = nc.scalar.activation(probs[:, h % 4, qt, :], probs[:, h % 4, qt, :], ACT.Exp,
                                                    bias=neg_max[:, g.par, j:j + 1], scale=SCALE,
                                                    accum_out=sums[:, g.par, j:j + 1])
                    last.then_inc(S["exp_ready"], 1)

                def pt_odd(g, h):
                    act.wait_ge(S["pt_ps"], g.count(H, h + 1))
                    wait(act, S["pv_done"], g.count(2, h // HG))
                    nc.scalar.activation(probs_t[:, h % 4, :], ps[:, BANK_PT + 1, :], ACT.Copy
                                         ).then_inc(S["pt_odd"], 1)

                def recip_t_copy(g):
                    act.wait_ge(S["recip_t_ps"], g.count(1, 1))
                    wait(act, S["o_ready"], g.count())
                    nc.scalar.activation(recip_t[:].rearrange("p t n -> p (t n)"), ps[:, BANK_X, :], ACT.Copy
                                         ).then_inc(S["recip_t_ready"], 1)

                def o_high(g):
                    act.wait_ge(S["o_ready"], g.count(1, 1))
                    wait(act, S["y_ps"], g.count())
                    nc.scalar.activation(o_parts[HIGH][:], o_t[:], ACT.Copy).then_inc(S["o_high"], 1)

                def step(g):
                    now, after, before = g.has(0), g.has(1), g.has(-1)
                    for h in range(H):
                        if h == 0 and after:
                            self.act_xt_high(act, g + 1, S["v_ps"])
                        if h == 0 and before:
                            exps(g + -1, H - 1)
                        if h >= 1 and now:
                            exps(g, h - 1)
                        if h == 1 and before:
                            pt_odd(g + -1, H - 1)
                        if h == 2 and after:
                            q_high(g + 1)
                        if h in (3, 5, 7) and now:
                            pt_odd(g, h - 2)
                        if h == 3 and before:
                            recip_t_copy(g + -1)
                        if h == 4 and after:
                            k_high(g + 1)
                        if h == 4 and before:
                            o_high(g + -1)
                        if h == 5 and after:
                            v_copy(g + 1)
                pipeline(act, step)

            def vector(self, dve):
                start_of_layer(dve, self.L)
                S = self.s

                def biased_low(parts, bank, bias, high, low, g):
                    dve.wait_ge(high, g.count(1, 1))
                    for ot in range(DT):
                        last = nc.vector.scalar_tensor_tensor(
                            out=parts[:, LOW, ot, :], in0=ps[:, bank, ot * N:(ot + 1) * N],
                            scalar=bias[:, ot:ot + 1], in1=parts[:, HIGH, ot, :].bitcast(F32),
                            op0=ALU.add, op1=ALU.subtract)
                    last.then_inc(low, 1)

                def masked_max(g, h):
                    dve.wait_ge(S["scores_ps"], g.count(H, h + 1))
                    wait(dve, S["pt_ps"], g.count(H, h - 3))
                    part(dve)
                    for qt in range(NT):
                        j = NT * h + qt
                        last = nc.vector.tensor_tensor_reduce(
                            probs[:, h % 4, qt, :], ps[:, BANK_S + h % 2, qt * N:(qt + 1) * N],
                            mask[:, qt, :], 1.0, LOWEST, ALU.add, ALU.max, maxes[:, g.par, j:j + 1])
                    last.then_inc(S["max_ready"], 1)
                    dve.wait_ge(S["max_ready"], g.count(H, h + 1))
                    nc.vector.tensor_scalar(neg_max[:, g.par, NT * h:NT * h + NT],
                                            maxes[:, g.par, NT * h:NT * h + NT], -SCALE, None, ALU.mult
                                            ).then_inc(S["neg_max_ready"], 1)

                def pt_even(g, h):
                    dve.wait_ge(S["pt_ps"], g.count(H, h + 1))
                    wait(dve, S["pv_done"], g.count(2, h // HG))
                    nc.vector.tensor_copy(probs_t[:, h % 4, :], ps[:, BANK_PT, :]).then_inc(S["pt_even"], 1)

                def recip_sums(g):
                    dve.wait_ge(S["exp_ready"], g.count(H, H))
                    nc.vector.reciprocal(recip[:], sums[:, g.par, :]).then_inc(S["recip_ready"], 1)
                    dve.wait_ge(S["recip_ready"], g.count(1, 1))
                    wait(dve, S["recip_t_ps"], g.count())
                    r = recip[:].rearrange("p (h q) -> p h q", q=NT)
                    for qt in range(NT):
                        last = nc.vector.tensor_scalar(recip_rep[:, qt].rearrange("p (h d) -> p h d", h=H),
                                                       r[:, :, qt:qt + 1].to_broadcast([P, H, DH]),
                                                       defined[:, qt:qt + 1], None, ALU.mult)
                    last.then_inc(S["recip_rep_ready"], 1)

                def normalize_o(g):
                    dve.wait_ge(S["pv_done"], g.count(2, 2))
                    dve.wait_ge(S["recip_t_ready"], g.count(1, 1))
                    wait(dve, S["o_low"], g.count())
                    nc.vector.tensor_tensor(o_t[:].rearrange("p t n -> p (t n)"), ps[:, BANK_O, :],
                                            recip_t[:].rearrange("p t n -> p (t n)"), ALU.mult
                                            ).then_inc(S["o_ready"], 1)

                def y_sum(g):
                    dve.wait_ge(S["y_ps"], g.count(1, 1))
                    dve.wait_ge(S["xb_ready"], g.count(1, 1))
                    nc.vector.tensor_tensor(y_sb[:].rearrange("p t d -> p (t d)"), ps[:, BANK_PROJ + 1, :],
                                            xb[:, g.par, :], ALU.add).then_inc(S["y_summed"], 1)

                def step(g):
                    now, after, before = g.has(0), g.has(1), g.has(-1)
                    for h in range(H):
                        if h == 0 and after:
                            self.dve_xt_low(dve, g + 1)
                        if now:
                            masked_max(g, h)
                        if h == 0 and before:
                            pt_even(g + -1, H - 2)
                        if h in (2, 4, 6) and now:
                            pt_even(g, h - 2)
                        if h == 1 and before:
                            recip_sums(g + -1)
                        if h == 3 and after:
                            biased_low(q_parts[:], BANK_PROJ, bias_q[self.L], S["q_high"], S["q_low"], g + 1)
                        if h == 3 and before:
                            normalize_o(g + -1)
                        if h == 4 and after:
                            biased_low(k_parts[(g + 1).par][:], BANK_PROJ + 1, bias_k[self.L], S["k_high"],
                                       S["k_low"], g + 1)
                        if h == 6 and before:
                            y_sum(g + -1)
                            self.dve_stats(dve, g + -1)
                        if h == 7 and before:
                            self.dve_normalize(dve, g + -1)
                pipeline(dve, step)

        class GraphAttention(Layer):

            def __init__(self, L):
                super().__init__(L, ["dst_ps", "max_ready", "wh_ps", "wh_ready", "src_max", "row_max", "neg_max",
                                     "summed", "logits_ready", "exp_ready", "pt_ps", "pt_ready",
                                     "recip_raw", "recip_ready"])

            def sync(self, sp):
                start_of_layer(sp, self.L)

                def step(g):
                    if g.has(2):
                        self.load(sp, g + 2)
                    if g.has(-2):
                        self.store(sp, g + -2)
                pipeline(sp, step)

            def gpsimd(self, pool):
                start_of_layer(pool, self.L)

                def step(g):
                    if g.has(1):
                        self.pool_xb(pool, g + 1, None)
                    if g.has(-1):
                        self.pool_rstd(pool, g + -1)
                pipeline(pool, step)

            def tensor(self, pe):
                start_of_layer(pe, self.L)
                S = self.s

                def dst_rows(g):
                    pe.wait_ge(S["xt_high"], g.count(1, 1))
                    pe.wait_ge(S["xt_low"], g.count(1, 1))
                    wait(pe, S["max_ready"], g.count())
                    three_pass(ps[:, 1, 0:N],
                               [([dst_rep[p][:, kt, :] for p in (0, 1)], [xt[p][:, kt, :] for p in (0, 1)])
                                for kt in range(DT)]).then_inc(S["dst_ps"], 1)

                def wh(g):
                    wait(pe, S["wh_ready"], g.count())
                    for nt in range(NT):
                        last = three_pass(ps[:, 2 + nt, 0:WE],
                                          [([xt[p][:, kt, nt * P:(nt + 1) * P] for p in (0, 1)],
                                            [w2[p][:, kt, :] for p in (0, 1)]) for kt in range(DT)])
                    last.then_inc(S["wh_ps"], 1)

                def transpose_probs(g):
                    pe.wait_ge(S["exp_ready"], g.count(1, 1))
                    wait(pe, S["pt_ready"], g.count())
                    for mt in range(NT):
                        for nt in range(NT):
                            last = nc.tensor.transpose(ps[:, 4, mt * N + nt * P:mt * N + (nt + 1) * P],
                                                       probs[:, 2, nt, mt * P:(mt + 1) * P], ident[:])
                    last.then_inc(S["pt_ps"], 1)

                def weighted_sum(g):
                    pe.wait_ge(S["pt_ready"], g.count(1, 1))
                    pe.wait_ge(S["wh_ready"], g.count(1, 1))
                    wait(pe, S["y_summed"], g.count(1, -1))
                    for nt in range(NT):
                        for mt in range(NT):
                            last = nc.tensor.matmul(ps[:, 6 + g.par, nt * D:(nt + 1) * D],
                                                    probs_t[:, 0, mt * N + nt * P:mt * N + (nt + 1) * P],
                                                    v_sb[:, g.par, mt, 0:D], start=(mt == 0), stop=(mt == NT - 1))
                    last.then_inc(S["y_ps"], 1)

                def step(g):
                    if g.has(1):
                        self.pe_transpose_x(pe, g + 1)
                    if g.has(0):
                        dst_rows(g)
                    if g.has(-1):
                        transpose_probs(g + -1)
                    if g.has(0):
                        wh(g)
                    if g.has(-1):
                        weighted_sum(g + -1)
                pipeline(pe, step)

            def scalar(self, act):
                start_of_layer(act, self.L)
                S = self.s

                def wh_copy(g):
                    act.wait_ge(S["wh_ps"], g.count(1, 1))
                    wait(act, S["y_ps"], g.count(1, -1))
                    nc.scalar.activation(v_sb[:, g.par, :, :], ps[:, 2:4, 0:WE], ACT.Copy
                                         ).then_inc(S["wh_ready"], 1)

                def exps(g):
                    act.wait_ge(S["logits_ready"], g.count(1, 1))
                    act.wait_ge(S["neg_max"], g.count(1, 1))
                    for nt in range(NT):
                        last = nc.scalar.activation(probs[:, 2, nt, :], probs[:, 2, nt, :], ACT.Exp,
                                                    bias=node_max[:, 2, nt:nt + 1],
                                                    accum_out=sums[:, g.par, nt:nt + 1])
                    last.then_inc(S["exp_ready"], 1)

                def step(g):
                    if g.has(0):
                        wh_copy(g)
                    if g.has(1):
                        self.act_xt_high(act, g + 1, S["wh_ps"])
                    if g.has(0):
                        exps(g)
                pipeline(act, step)

            def vector(self, dve):
                start_of_layer(dve, self.L)
                S = self.s

                def masked_max(g):
                    dve.wait_ge(S["dst_ps"], g.count(1, 1))
                    part(dve)
                    for nt in range(NT):
                        last = nc.vector.tensor_tensor_reduce(probs[:, 0, nt, :], ps[:, 1, 0:N], mask[:, nt, :],
                                                              1.0, LOWEST, ALU.add, ALU.max,
                                                              maxes[:, g.par, nt:nt + 1])
                    last.then_inc(S["max_ready"], 1)

                def pt_copy(g):
                    dve.wait_ge(S["pt_ps"], g.count(1, 1))
                    wait(dve, S["y_ps"], g.count())
                    nc.vector.tensor_scalar(probs_t[:, 0, :], ps[:, 4, :], 0.0, None, ALU.max
                                            ).then_inc(S["pt_ready"], 1)

                def recip_sums(g):
                    dve.wait_ge(S["exp_ready"], g.count(1, 1))
                    nc.vector.reciprocal(src_recip[:, 0, :], sums[:, g.par, 0:NT]).then_inc(S["recip_raw"], 1)
                    dve.wait_ge(S["recip_raw"], g.count(1, 1))
                    nc.vector.scalar_tensor_tensor(out=src_recip[:, 1, :], in0=src_recip[:, 0, :], scalar=0.0,
                                                   in1=row_any[:], op0=ALU.max, op1=ALU.mult
                                                   ).then_inc(S["recip_ready"], 1)

                def logits(g):
                    e_src = v_sb[:, g.par, :, D]
                    dve.wait_ge(S["wh_ready"], g.count(1, 1))
                    dve.wait_ge(S["max_ready"], g.count(1, 1))
                    wait(dve, S["exp_ready"], g.count())
                    nc.vector.tensor_tensor(node_max[:, 0, :], maxes[:, g.par, 0:NT], e_src, ALU.add
                                            ).then_inc(S["src_max"], 1)
                    for nt in range(NT):
                        last = nc.vector.tensor_scalar(probs[:, 1, nt, :], probs[:, 0, nt, :],
                                                       v_sb[:, g.par, nt, D:D + 1], None, ALU.add)
                    last.then_inc(S["summed"], 1)
                    dve.wait_ge(S["src_max"], g.count(1, 1))
                    nc.vector.scalar_tensor_tensor(out=node_max[:, 1, :], in0=node_max[:, 0, :], scalar=NEG_SLOPE,
                                                   in1=node_max[:, 0, :], op0=ALU.mult, op1=ALU.max
                                                   ).then_inc(S["row_max"], 1)
                    dve.wait_ge(S["summed"], g.count(1, 1))
                    wait(dve, S["pt_ps"], g.count())
                    nc.vector.scalar_tensor_tensor(out=probs[:, 2].rearrange("p t n -> p (t n)"),
                                                   in0=probs[:, 1].rearrange("p t n -> p (t n)"),
                                                   scalar=NEG_SLOPE,
                                                   in1=probs[:, 1].rearrange("p t n -> p (t n)"),
                                                   op0=ALU.mult, op1=ALU.max).then_inc(S["logits_ready"], 1)
                    dve.wait_ge(S["row_max"], g.count(1, 1))
                    nc.vector.tensor_scalar(node_max[:, 2, :], node_max[:, 1, :], -1.0, None, ALU.mult
                                            ).then_inc(S["neg_max"], 1)

                def y_sum(g):
                    dve.wait_ge(S["y_ps"], g.count(1, 1))
                    dve.wait_ge(S["xb_ready"], g.count(1, 1))
                    dve.wait_ge(S["recip_ready"], g.count(1, 1))
                    for nt in range(NT):
                        last = nc.vector.scalar_tensor_tensor(
                            out=y_sb[:, nt, :], in0=ps[:, 6 + g.par, nt * D:(nt + 1) * D],
                            scalar=src_recip[:, 1, nt:nt + 1], in1=xb[:, g.par, nt * D:(nt + 1) * D],
                            op0=ALU.mult, op1=ALU.add)
                    last.then_inc(S["y_summed"], 1)

                def step(g):
                    if g.has(-2):
                        self.dve_normalize(dve, g + -2)
                    if g.has(0):
                        masked_max(g)
                    if g.has(-1):
                        recip_sums(g + -1)
                        pt_copy(g + -1)
                    if g.has(1):
                        self.dve_xt_low(dve, g + 1)
                    if g.has(0):
                        logits(g)
                    if g.has(-1):
                        y_sum(g + -1)
                        self.dve_stats(dve, g + -1)
                pipeline(dve, step)

        layers = [MessagePassing(0), Attention(1), GraphAttention(2), Attention(3)]

        block = ctx.enter_context(nc.Block())

        @block.sync
        def _(sp):
            prep_sync(sp)
            for layer in layers:
                layer.sync(sp)
            sp.wait_ge(layer_done[3][0], 16 * (B // 2))
            sp.wait_ge(layer_done[3][1], 16 * (B // 2))

        @block.gpsimd
        def _(pool):
            prep_gpsimd(pool)
            for layer in layers:
                layer.gpsimd(pool)

        @block.tensor
        def _(pe):
            prep_tensor(pe)
            for layer in layers:
                layer.tensor(pe)

        @block.scalar
        def _(act):
            prep_scalar(act)
            for layer in layers:
                layer.scalar(act)

        @block.vector
        def _(dve):
            prep_vector(dve)
            for layer in layers:
                layer.vector(dve)


_INS = ["x", "adj", "L0_gnn_W", "L0_gnn_b", "L1_gnn_Wq", "L1_gnn_bq", "L1_gnn_Wk", "L1_gnn_bk", "L1_gnn_Wv",
        "L1_gnn_bv", "L1_gnn_Wo", "L1_gnn_bo", "L2_gnn_W", "L2_gnn_a_src", "L2_gnn_a_dst", "L3_gnn_Wq",
        "L3_gnn_bq", "L3_gnn_Wk", "L3_gnn_bk", "L3_gnn_Wv", "L3_gnn_bv", "L3_gnn_Wo", "L3_gnn_bo"]


def kernel(**inputs):
    import numpy as _np
    import concourse.bacc as _bacc
    from concourse import mybir as _mybir
    from concourse.bass_utils import run_bass_kernel_spmd as _run

    nc = _bacc.Bacc("TRN2", target_bir_lowering=False, num_devices=1)
    arrays, args = {}, []
    for name in _INS:
        a = _np.ascontiguousarray(inputs[name])
        arrays[f"in_{name}"] = a
        args.append(nc.dram_tensor(f"in_{name}", a.shape, _mybir.dt.from_np(a.dtype), kind="ExternalInput").ap())
    args.append(nc.dram_tensor("out_y", (B, N, D), _mybir.dt.float32, kind="ExternalOutput").ap())
    graph_layers_kernel(nc, *args)
    r = _run(nc, [arrays], core_ids=[0])
    return r.results[0]["out_y"]
```

```python
import concourse.bass as bass
from concourse import mybir
from contextlib import ExitStack

F32 = mybir.dt.float32
F32R = mybir.dt.float32r
I32 = mybir.dt.int32
ACT = mybir.ActivationFunctionType
ALU = mybir.AluOpType
AX = mybir.AxisListType

P = 128
B, N, D = 32, 256, 256
NT = N // P
DT = D // P
H = 8
DH = D // H
HG = P // DH
SCALE = DH ** -0.5
EPS = 1e-5
NEG_SLOPE = 0.2
MASKED = -1.0e38
LOWEST, HIGHEST = -3.0e38, 3.0e38
WE = D + 2
HIGH, LOW = 0, 1


class Graph:

    def __init__(self, t, par):
        self.t, self.par = t, par

    def __add__(self, n):
        k = self.par + n
        return Graph(self.t + k // 2, k % 2)

    def has(self, n):
        return not isinstance(self.t, int) or 0 <= 2 * self.t + self.par + n < B

    def count(self, k=1, c=0):
        return self.t * (2 * k) + (self.par * k + c)

    def turns(self, k=1, c=0):
        return self.t * k + c


def wait(eng, sem, value):
    if not isinstance(value, int) or value > 0:
        eng.wait_ge(sem, value)


def pipeline(eng, step):
    for n in range(-2, 4):
        step(Graph(n // 2, n % 2))
    with eng.Fori(0, (B - 6) // 2) as t:
        step(Graph(t + 2, 0))
        step(Graph(t + 2, 1))
    for n in range(B - 2, B + 4):
        step(Graph(n // 2, n % 2))


def graph_layers_kernel(nc, x, adj, L0_W, L0_b, L1_Wq, L1_bq, L1_Wk, L1_bk, L1_Wv, L1_bv, L1_Wo, L1_bo,
                        L2_W, L2_a_src, L2_a_dst,
                        L3_Wq, L3_bq, L3_Wk, L3_bk, L3_Wv, L3_bv, L3_Wo, L3_bo, out):
    ctx = ExitStack()
    with ctx:
        def sb(name, shape, dt=F32):
            return ctx.enter_context(nc.sbuf_tensor(name, shape, dt))

        def sem(name):
            return ctx.enter_context(nc.semaphore(name))

        x_res = sb("x_res", [P, B, NT * D])
        ident = sb("ident", [P, P])
        mask = sb("mask", [P, NT, N])
        row_any = sb("row_any", [P, NT])
        defined = sb("defined", [P, NT])
        deg = sb("deg", [P, NT])
        w0 = [sb(f"w0_{p}", [P, DT, 2 * D], F32R) for p in "hl"]
        wt = {(L, n): [sb(f"w{L}{n}_{p}", [P, DT, D], F32R) for p in "hl"] for L in (1, 3) for n in "qkvo"}
        w2 = [sb(f"w2_{p}", [P, DT, WE], F32R) for p in "hl"]
        dst_rep = [sb(f"dst_rep_{p}", [P, DT, P], F32R) for p in "hl"]
        bias_q = {L: sb(f"bias_q{L}", [P, DT]) for L in (1, 3)}
        bias_k = {L: sb(f"bias_k{L}", [P, DT]) for L in (1, 3)}
        bias_v = {L: sb(f"bias_v{L}", [P, DT]) for L in (1, 3)}
        bias_o = {L: sb(f"bias_o{L}", [P, D]) for L in (1, 3)}

        x_in = sb("x_in", [P, 2, NT * D])
        xt = [sb(f"xt_{p}", [P, DT, N], F32R) for p in "hl"]
        q_parts = sb("q_parts", [P, 2, DT, N], F32R)
        k_mixed = [sb(f"k_mixed{i}", [P, 2, DT, N], F32R) for i in range(2)]
        k_low_sb = sb("k_low_sb", [P, DT, N], F32R)
        qz = [sb(f"qz{i}", [P, HG, 2, DT, N], F32R) for i in range(2)]
        v_sb = sb("v_sb", [P, 2, NT, D])
        probs = sb("probs", [P, 4, NT, N])
        probs_t = sb("probs_t", [P, 4, NT * N])
        maxes = sb("maxes", [P, 2, NT])
        neg_max = sb("neg_max", [P, 2, 2 * H])
        sums = sb("sums", [P, 2, 2 * H])
        recip = sb("recip", [P, 2 * H])
        recip_rep = sb("recip_rep", [P, NT, D])
        recip_t = sb("recip_t", [P, DT, N])
        o_t = sb("o_t", [P, DT, N])
        o_parts = [sb(f"o_t_{p}", [P, DT, N], F32R) for p in "hl"]
        y_sb = sb("y_sb", [P, NT, D])
        y_out = sb("y_out", [P, 2, NT * D])
        node_max = sb("node_max", [P, 3, NT])
        e_src = sb("e_src", [P, 2, NT])
        neg_mean = sb("neg_mean", [P, NT])
        shift = sb("shift", [P, NT])
        src_recip = sb("src_recip", [P, 2, NT])
        stats = sb("stats", [P, NT, 6])
        mean_var = sb("mean_var", [P, NT, 2])
        var_eps = sb("var_eps", [P, NT])
        rstd = sb("rstd", [P, NT])
        minus_half = sb("minus_half", [P, NT])

        adj_t = recip_t
        deg_b = o_t
        y_pair = probs_t[:, 2:4, :].rearrange("p a (t d) -> p a t d", t=NT)

        ps = ctx.enter_context(nc.psum_tensor("ps", [P, 8, 512], F32))
        BANK_X, BANK_O, BANK_PROJ, BANK_S, BANK_PT = 0, 1, 2, 4, 6

        raw_names = ["0i", "0j", "1q", "1k", "1v", "1o", "3q", "3k", "3v", "3o"]
        raw_src = {"0i": L0_W[:, 0:D], "0j": L0_W[:, D:2 * D], "1q": L1_Wq, "1k": L1_Wk, "1v": L1_Wv,
                   "1o": L1_Wo, "3q": L3_Wq, "3k": L3_Wk, "3v": L3_Wv, "3o": L3_Wo}
        raw = {n: x_res[:, i, :].rearrange("p (t d) -> p t d", t=DT) for i, n in enumerate(raw_names)}
        raw2 = x_res[:, 10, :].rearrange("p (t d) -> p t d", t=DT)
        adj_i = x_res[:, 11, :].rearrange("p (t d) -> p t d", t=NT).bitcast(I32)
        adj_f = x_res[:, 20, :].rearrange("p (t n) -> p t n", t=NT)
        rows = {n: x_res[:, 12 + i, 0:D] for i, n in enumerate(["b0", "bo1", "bo3", "asrc", "adst"])}
        zeros = x_res[:, 17, 0:P]
        scratch = x_res[:, 18, 0:D]
        va = x_res[:, 19, 0:4]
        bv_rep = {L: [o_parts[p][:, :, 0:P] if L == 1 else o_parts[p][:, :, P:2 * P] for p in (0, 1)]
                  for L in (1, 3)}
        row_src = {"b0": L0_b, "bo1": L1_bo, "bo3": L3_bo, "asrc": L2_a_src, "adst": L2_a_dst}

        def weight_dst(n, p):
            if n == "0i":
                return w0[p][:, :, 0:D]
            if n == "0j":
                return w0[p][:, :, D:2 * D]
            return wt[(int(n[0]), n[1])][p][:, :, :]

        adj_loaded = sem("adj_loaded")
        weight_loaded = {n: sem(f"weight_loaded_{n}") for n in raw_names + ["2"]}
        rows_loaded = sem("rows_loaded")
        ident_ready = sem("ident_ready")
        consts_ready = sem("consts_ready")
        wt_transposed = sem("wt_transposed")
        wt_high = sem("wt_high")
        wt_low = sem("wt_low")
        prep_step = sem("prep_step")
        bias_product = sem("bias_product")
        qz_zeroed = sem("qz_zeroed")
        prepared = sem("prepared")
        apart = sem("apart")
        layer_done = [[sem(f"layer{L}_stored{p}") for p in range(2)] for L in range(4)]

        def start_of_layer(eng, L):
            if L == 0:
                eng.wait_ge(prepared, 1)
            else:
                eng.wait_ge(layer_done[L - 1][0], 16 * (B // 2))
                eng.wait_ge(layer_done[L - 1][1], 16 * (B // 2))

        def part(eng):
            eng.sem_inc(apart, 1)

        def three_pass(pe_out, pairs):
            n = len(pairs) * 3
            i = 0
            for st, mv in pairs:
                for a, b in ((HIGH, HIGH), (HIGH, LOW), (LOW, HIGH)):
                    last = nc.tensor.matmul(pe_out, st[a], mv[b], start=(i == 0), stop=(i == n - 1))
                    i += 1
            return last

        N_RAW = len(raw_names)

        def prep_sync(sp):
            sp.dma_start(raw["0i"], raw_src["0i"].rearrange("(t p) d -> p t d", p=P)).then_inc(weight_loaded["0i"], 16)
            sp.dma_start(adj_i, adj.rearrange("(t p) d -> p t d", p=P)).then_inc(adj_loaded, 16)
            for n in raw_names[1:]:
                sp.dma_start(raw[n], raw_src[n].rearrange("(t p) d -> p t d", p=P)).then_inc(weight_loaded[n], 16)
            sp.dma_start(raw2, L2_W.rearrange("(t p) d -> p t d", p=P)).then_inc(weight_loaded["2"], 16)
            for n, src in row_src.items():
                sp.dma_start(rows[n], src.partition_broadcast(P)).then_inc(rows_loaded, 16)
            for dst, src in ((bias_q[1], L1_bq), (bias_k[1], L1_bk), (bias_v[1], L1_bv),
                             (bias_q[3], L3_bq), (bias_k[3], L3_bk), (bias_v[3], L3_bv)):
                sp.dma_start(dst[:], src.rearrange("(t p) -> p t", p=P), allow_slow_non_contiguous=True).then_inc(rows_loaded, 16)

        def prep_gpsimd(pool):
            nc.gpsimd.memset(ident[:], 0.0).then_inc(ident_ready, 1)
            pool.wait_ge(ident_ready, 1)
            nc.gpsimd.affine_select(out=ident[:], in_=ident[:], compare_op=ALU.not_equal, fill=1.0, base=0,
                                    pattern=[[-1, P]], channel_multiplier=1).then_inc(ident_ready, 1)
            nc.gpsimd.memset(zeros, 0.0).then_inc(consts_ready, 1)
            nc.gpsimd.memset(minus_half[:], -0.5).then_inc(consts_ready, 1)
            for i in range(2):
                nc.gpsimd.memset(qz[i][:].bitcast(F32).rearrange("p a b c d -> p (a b c d)"), 0.0).then_inc(qz_zeroed, 1)

        def prep_tensor(pe):
            pe.wait_ge(ident_ready, 2)
            for i, n in enumerate(raw_names):
                pe.wait_ge(weight_loaded[n], 16)
                wait(pe, wt_low, i - 3)
                for dt in range(DT):
                    for ot in range(DT):
                        last = nc.tensor.transpose(ps[:, i % 4, dt * D + ot * P:dt * D + (ot + 1) * P],
                                                   raw[n][:, ot, dt * P:(dt + 1) * P], ident[:])
                last.then_inc(wt_transposed, 1)
            pe.wait_ge(prep_step, 1)
            for jt in range(NT):
                for it in range(NT):
                    last = nc.tensor.transpose(ps[:, 4, jt * N + it * P:jt * N + (it + 1) * P],
                                               adj_f[:, it, jt * P:(jt + 1) * P], ident[:])
            last.then_inc(wt_transposed, 1)
            pe.wait_ge(wt_low, N_RAW)
            pe.wait_ge(consts_ready, 4)
            for L in (1, 3):
                last = three_pass(ps[:, 5 + L // 2, 0:D],
                                  [([bv_rep[L][p][:, ct, :] for p in (0, 1)],
                                    [wt[(L, "o")][p][:, ct, :] for p in (0, 1)]) for ct in range(DT)])
            last.then_inc(bias_product, 1)

        def prep_scalar(act):
            for i, n in enumerate(raw_names):
                act.wait_ge(wt_transposed, i + 1)
                nc.scalar.activation(weight_dst(n, HIGH), ps[:, i % 4, :].rearrange("p (t d) -> p t d", t=DT),
                                     ACT.Copy).then_inc(wt_high, 1)

        def prep_vector(dve):
            done = [0]

            def link(ins):
                done[0] += 1
                ins.then_inc(prep_step, 1)
                dve.wait_ge(prep_step, done[0])

            dve.wait_ge(adj_loaded, 16)
            link(nc.vector.tensor_copy(adj_f, adj_i))
            for i, n in enumerate(raw_names):
                dve.wait_ge(wt_high, i + 1)
                nc.vector.tensor_tensor(weight_dst(n, LOW), ps[:, i % 4, :].rearrange("p (t d) -> p t d", t=DT),
                                        weight_dst(n, HIGH).bitcast(F32), ALU.subtract).then_inc(wt_low, 1)
            link(nc.vector.reduce_sum(deg[:], adj_f, AX.X))
            link(nc.vector.tensor_scalar(mask[:], adj_f, 0.0, MASKED, ALU.is_equal, ALU.mult))
            link(nc.vector.reduce_max(row_any[:], mask[:], AX.X))
            link(nc.vector.tensor_scalar(row_any[:], row_any[:], 0.0, None, ALU.is_equal))
            link(nc.vector.reciprocal(defined[:], row_any[:]))
            link(nc.vector.tensor_tensor(defined[:], defined[:], row_any[:], ALU.mult))
            dve.wait_ge(wt_transposed, N_RAW + 1)
            link(nc.vector.tensor_copy(adj_t[:].rearrange("p t n -> p (t n)"), ps[:, 4, :]))
            dve.wait_ge(rows_loaded, 16 * 11)
            for nt in range(NT):
                link(nc.vector.tensor_scalar(deg_b[:, nt, :], rows["b0"], deg[:, nt:nt + 1], None, ALU.mult))
            dve.wait_ge(weight_loaded["2"], 16)
            for i, row in enumerate(("asrc", "adst")):
                for dt in range(DT):
                    link(nc.vector.tensor_tensor_reduce(scratch, raw2[:, dt, :], rows[row], 1.0, 0.0,
                                                        ALU.mult, ALU.add, va[:, 2 * i + dt:2 * i + dt + 1]))
            dve.wait_ge(consts_ready, 2)
            link(nc.vector.tensor_copy(w2[HIGH][:, :, 0:D], raw2))
            link(nc.vector.tensor_tensor(w2[LOW][:, :, 0:D], raw2, w2[HIGH][:, :, 0:D].bitcast(F32), ALU.subtract))

            def split_column(high, low, col, n):
                link(nc.vector.tensor_scalar(high, zeros[:, 0:n], col, None, ALU.add))
                return nc.vector.scalar_tensor_tensor(out=low, in0=zeros[:, 0:n], scalar=col,
                                                      in1=high.bitcast(F32), op0=ALU.add, op1=ALU.subtract)

            for dt in range(DT):
                link(split_column(w2[HIGH][:, dt, D:WE], w2[LOW][:, dt, D:WE], va[:, dt:dt + 1], WE - D))
                link(split_column(dst_rep[HIGH][:, dt, :], dst_rep[LOW][:, dt, :], va[:, 2 + dt:3 + dt], P))
                for L in (1, 3):
                    link(split_column(bv_rep[L][HIGH][:, dt, :], bv_rep[L][LOW][:, dt, :],
                                      bias_v[L][:, dt:dt + 1], P))
            link(nc.vector.tensor_copy(scratch, rows["bo1"]))
            nc.vector.tensor_copy(scratch, rows["bo3"]).then_inc(consts_ready, 2)
            dve.wait_ge(bias_product, 1)
            link(nc.vector.tensor_tensor(bias_o[1][:], ps[:, 5, 0:D], rows["bo1"], ALU.add))
            nc.vector.tensor_tensor(bias_o[3][:], ps[:, 6, 0:D], rows["bo3"], ALU.add).then_inc(prepared, 1)

        class Layer:

            def __init__(self, L, names, loops=()):
                self.L = L
                shared = ["xt_ps", "xt_high", "xt_low", "xb_ready", "y_ps", "y_summed", "y_stats", "y_var",
                          "var_eps_ready", "rstd_ready", "out_ready"]
                self.s = {n: sem(f"L{L}_{n}") for n in shared + names}
                self.x_loaded = [sem(f"L{L}_x_loaded{p}") for p in range(2)]
                self.stored = layer_done[L]

            def load(self, sp, g):
                wait(sp, self.s["xt_ps"], g.count(1, -1))
                if self.L != 2:
                    wait(sp, self.s["xb_ready"], g.count(1, -1))
                dst = x_in[:, g.par, :]
                if self.L == 0:
                    sp.dma_start(dst.rearrange("p (t d) -> p t d", t=NT),
                                 x.rearrange("b (t p) d -> p (b t) d", p=P)[:, bass.ds(g.count(NT), NT), :]
                                 ).then_inc(self.x_loaded[g.par], 16)
                else:
                    sp.dma_start(dst, x_res[:, bass.ds(g.count(), 1), :].rearrange("p a n -> p (a n)")
                                 ).then_inc(self.x_loaded[g.par], 16)

            def store(self, sp, g):
                sp.wait_ge(self.s["out_ready"], g.count(1, 1))
                src = y_out[:, g.par, :]
                if self.L == 3:
                    sp.dma_start(out.rearrange("b (t p) d -> p (b t) d", p=P)[:, bass.ds(g.count(NT), NT), :],
                                 src.rearrange("p (t d) -> p t d", t=NT)).then_inc(self.stored[g.par], 16)
                else:
                    sp.dma_start(x_res[:, bass.ds(g.count(), 1), :].rearrange("p a n -> p (a n)"), src
                                 ).then_inc(self.stored[g.par], 16)

            def pe_transpose_x(self, pe, g):
                pe.wait_ge(self.x_loaded[g.par], g.turns(16, 16))
                wait(pe, self.s["xt_low"], g.count())
                for dt in range(DT):
                    for nt in range(NT):
                        last = nc.tensor.transpose(
                            ps[:, BANK_X, dt * N + nt * P:dt * N + (nt + 1) * P],
                            x_in[:, g.par, nt * D + dt * P:nt * D + (dt + 1) * P], ident[:])
                last.then_inc(self.s["xt_ps"], 1)

            def act_xt_high(self, act, g, xt_used):
                act.wait_ge(self.s["xt_ps"], g.count(1, 1))
                wait(act, xt_used, g.count(1, 0 if self.L in (1, 3) else -1))
                nc.scalar.activation(self.xt(g)[HIGH].rearrange("p t n -> p (t n)"), ps[:, BANK_X, :], ACT.Copy
                                     ).then_inc(self.s["xt_high"], 1)

            def dve_xt_low(self, dve, g):
                dve.wait_ge(self.s["xt_high"], g.count(1, 1))
                nc.vector.tensor_tensor(self.xt(g)[LOW].rearrange("p t n -> p (t n)"), ps[:, BANK_X, :],
                                        self.xt(g)[HIGH].bitcast(F32).rearrange("p t n -> p (t n)"),
                                        ALU.subtract).then_inc(self.s["xt_low"], 1)

            def xt(self, g):
                if self.L in (1, 3) or g.par == 0:
                    return [xt[HIGH][:], xt[LOW][:]]
                return [k_mixed[0][:, HIGH], k_mixed[0][:, LOW]]

            def y(self, g):
                return y_pair[:, g.par] if self.L == 2 else y_sb

            def dve_stats(self, dve, g):
                dve.wait_ge(self.s["y_summed"], g.count(1, 1))
                for nt in range(NT):
                    last = nc.vector.bn_stats(stats[:, nt, :], self.y(g)[:, nt, :])
                last.then_inc(self.s["y_stats"], 1)
                dve.wait_ge(self.s["y_stats"], g.count(1, 1))
                wait(dve, self.s["rstd_ready"], g.count())
                if self.L == 2:
                    wait(dve, self.s["shift_ready"], g.count())
                part(dve)
                for nt in range(NT):
                    last = nc.vector.bn_aggr(mean_var[:, nt, :], stats[:, nt, :])
                last.then_inc(self.s["y_var"], 1)

            def pool_rstd(self, pool, g):
                pool.wait_ge(self.s["y_var"], g.count(1, 1))
                part(pool)
                nc.gpsimd.tensor_scalar(var_eps[:], mean_var[:, :, 1], EPS, 1.0, ALU.add, ALU.mult
                                        ).then_inc(self.s["var_eps_ready"], 1)
                pool.wait_ge(self.s["var_eps_ready"], g.count(1, 1))
                wait(pool, self.s["out_ready"], g.count())
                nc.gpsimd.tensor_tensor(rstd[:], var_eps[:], minus_half[:], ALU.pow
                                        ).then_inc(self.s["rstd_ready"], 1)

            def dve_normalize(self, dve, g):
                dve.wait_ge(self.s["rstd_ready"], g.count(1, 1))
                wait(dve, self.stored[g.par], g.turns(16))
                for nt in range(NT):
                    last = nc.vector.tensor_scalar(y_out[:, g.par, nt * D:(nt + 1) * D], self.y(g)[:, nt, :],
                                                   mean_var[:, nt, 0:1], rstd[:, nt:nt + 1],
                                                   ALU.subtract, ALU.mult)
                last.then_inc(self.s["out_ready"], 1)

            def pool_shift(self, pool, g):
                nc.gpsimd.tensor_scalar(neg_mean[:], mean_var[:, :, 0], -1.0, 1.0, ALU.mult, ALU.mult
                                        ).then_inc(self.s["neg_mean_ready"], 1)
                pool.wait_ge(self.s["neg_mean_ready"], g.count(1, 1))
                pool.wait_ge(self.s["rstd_ready"], g.count(1, 1))
                nc.gpsimd.tensor_tensor(shift[:], neg_mean[:], rstd[:], ALU.mult
                                        ).then_inc(self.s["shift_ready"], 1)

            def act_normalize(self, act, g):
                act.wait_ge(self.s["shift_ready"], g.count(1, 1))
                wait(act, self.stored[g.par], g.turns(16))
                for nt in range(NT):
                    last = nc.scalar.activation(y_out[:, g.par, nt * D:(nt + 1) * D], self.y(g)[:, nt, :],
                                                ACT.Identity, bias=shift[:, nt:nt + 1], scale=rstd[:, nt:nt + 1])
                last.then_inc(self.s["out_ready"], 1)

            def x_of(self, g, tiles=slice(0, NT)):
                return x_res[:, bass.ds(g.count(), 1), tiles.start * D:tiles.stop * D].rearrange("p a n -> p (a n)")

            def pool_xb(self, pool, g, const):
                pool.wait_ge(self.x_loaded[g.par], g.turns(16, 16))
                part(pool)
                for nt in range(NT):
                    s = slice(nt * D, (nt + 1) * D)
                    last = nc.gpsimd.tensor_tensor(self.x_of(g, slice(nt, nt + 1)), x_in[:, g.par, s], const[nt],
                                                   ALU.add)
                last.then_inc(self.s["xb_ready"], 1)

        class MessagePassing(Layer):
            def __init__(self, L):
                super().__init__(L, ["m_ps", "mj_ready", "mi_scaled"])

            def sync(self, sp):
                start_of_layer(sp, self.L)

                def step(g):
                    if g.has(2):
                        self.load(sp, g + 2)
                    if g.has(-3):
                        self.store(sp, g + -3)
                pipeline(sp, step)

            def gpsimd(self, pool):
                start_of_layer(pool, self.L)

                def step(g):
                    if g.has(1):
                        self.pool_xb(pool, g + 1, [deg_b[:, nt, :] for nt in range(NT)])
                    if g.has(-2):
                        self.pool_rstd(pool, g + -2)
                pipeline(pool, step)

            def tensor(self, pe):
                start_of_layer(pe, self.L)
                S = self.s

                def products(g):
                    pe.wait_ge(S["xt_high"], g.count(1, 1))
                    pe.wait_ge(S["xt_low"], g.count(1, 1))
                    wait(pe, S["mi_scaled"], g.count(1, -1))
                    for nt in range(NT):
                        last = three_pass(ps[:, 2 + 2 * g.par + nt, :],
                                          [([self.xt(g)[p][:, kt, nt * P:(nt + 1) * P] for p in (0, 1)],
                                            [w0[p][:, kt, :] for p in (0, 1)]) for kt in range(DT)])
                    last.then_inc(S["m_ps"], 1)

                def mix(g):
                    pe.wait_ge(S["mj_ready"], g.count(1, 1))
                    wait(pe, S["y_summed"], g.count(1, -1))
                    for it in range(NT):
                        for jt in range(NT):
                            last = nc.tensor.matmul(ps[:, 6 + g.par, it * D:(it + 1) * D],
                                                    adj_t[:, jt, it * P:(it + 1) * P],
                                                    v_sb[:, g.par, jt, :], start=(jt == 0), stop=(jt == NT - 1))
                    last.then_inc(S["y_ps"], 1)

                def step(g):
                    if g.has(1):
                        self.pe_transpose_x(pe, g + 1)
                    if g.has(0):
                        products(g)
                    if g.has(-1):
                        mix(g + -1)
                pipeline(pe, step)

            def scalar(self, act):
                start_of_layer(act, self.L)
                S = self.s

                def step(g):
                    if g.has(1):
                        self.act_xt_high(act, g + 1, S["m_ps"])
                    if g.has(0):
                        act.wait_ge(S["m_ps"], g.count(1, 1))
                        wait(act, S["y_ps"], g.count(1, -1))
                        nc.scalar.activation(v_sb[:, g.par, :, :],
                                             ps[:, 2 + 2 * g.par:4 + 2 * g.par, D:2 * D], ACT.Copy
                                             ).then_inc(S["mj_ready"], 1)
                pipeline(act, step)

            def vector(self, dve):
                start_of_layer(dve, self.L)
                S = self.s

                def scale_mi(g):
                    dve.wait_ge(S["mj_ready"], g.count(1, 1))
                    dve.wait_ge(S["xb_ready"], g.count(1, 1))
                    for nt in range(NT):
                        last = nc.vector.scalar_tensor_tensor(
                            out=probs[:, g.par, nt, :], in0=ps[:, 2 + 2 * g.par + nt, 0:D],
                            scalar=deg[:, nt:nt + 1], in1=self.x_of(g, slice(nt, nt + 1)),
                            op0=ALU.mult, op1=ALU.add)
                    last.then_inc(S["mi_scaled"], 1)

                def y_sum(g):
                    dve.wait_ge(S["y_ps"], g.count(1, 1))
                    dve.wait_ge(S["mi_scaled"], g.count(1, 1))
                    wait(dve, S["out_ready"], g.count())
                    nc.vector.tensor_tensor(y_sb[:].rearrange("p t d -> p (t d)"), ps[:, 6 + g.par, :],
                                            probs[:, g.par, :, :].rearrange("p t d -> p (t d)"), ALU.add
                                            ).then_inc(S["y_summed"], 1)

                def step(g):
                    if g.has(-3):
                        self.dve_normalize(dve, g + -3)
                    if g.has(1):
                        self.dve_xt_low(dve, g + 1)
                    if g.has(-2):
                        y_sum(g + -2)
                        self.dve_stats(dve, g + -2)
                    if g.has(0):
                        scale_mi(g)
                pipeline(dve, step)

        class Attention(Layer):

            def __init__(self, L):
                super().__init__(L, ["q_ps", "k_ps", "v_ps", "q_high", "q_low", "k_high", "k_copied", "k_low", "v_ready",
                                     "scores_ps", "max_ready", "exp_ready",
                                     "pt_ps",
                                     "pt_even", "pt_odd",
                                     "pv_done",
                                     "recip_ready", "recip_rep_ready", "recip_t_ps", "recip_t_ready",
                                     "o_ready", "o_high", "o_low"])
                self.qz_ready = [sem(f"L{L}_qz_ready{p}") for p in range(2)]
                self.k_mixed_ready = [sem(f"L{L}_k_mixed_ready{p}") for p in range(2)]

            def sync(self, sp):
                start_of_layer(sp, self.L)
                sp.wait_ge(qz_zeroed, 2)
                S = self.s

                def spread_q(g):
                    sp.wait_ge(S["q_low"], g.count(1, 1))
                    part(sp)
                    wait(sp, S["scores_ps"], g.count(H, -H))
                    for a in range(HG):
                        rows_a = slice(a * DH, (a + 1) * DH)
                        beside = slice((a ^ 1) * DH, ((a ^ 1) + 1) * DH)
                        sp.dma_start(qz[g.par][rows_a, a].bitcast(F32).rearrange("p a t n -> p (a t n)"),
                                     q_parts[rows_a].bitcast(F32).rearrange("p a t n -> p (a t n)")
                                     ).then_inc(self.qz_ready[g.par], 16)
                        sp.dma_start(qz[g.par][beside, a, HIGH].bitcast(F32).rearrange("p t n -> p (t n)"),
                                     q_parts[rows_a, HIGH].bitcast(F32).rearrange("p t n -> p (t n)")
                                     ).then_inc(self.qz_ready[g.par], 16)

                def mix_k(g):
                    sp.wait_ge(S["k_low"], g.count(1, 1))
                    sp.wait_ge(S["k_copied"], g.count(1, 1))
                    for a in range(HG):
                        rows_a = slice(a * DH, (a + 1) * DH)
                        beside = slice((a ^ 1) * DH, ((a ^ 1) + 1) * DH)
                        sp.dma_start(k_mixed[g.par][beside, a % 2].bitcast(F32).rearrange("p t n -> p (t n)"),
                                     k_low_sb[rows_a].bitcast(F32).rearrange("p t n -> p (t n)")
                                     ).then_inc(self.k_mixed_ready[g.par], 16)

                def step(g):
                    if g.has(2):
                        self.load(sp, g + 2)
                    if g.has(1):
                        spread_q(g + 1)
                        mix_k(g + 1)
                    if g.has(-2):
                        self.store(sp, g + -2)
                pipeline(sp, step)

            def gpsimd(self, pool):
                start_of_layer(pool, self.L)
                S = self.s

                def k_copy(g):
                    pool.wait_ge(S["k_high"], g.count(1, 1))
                    part(pool)
                    nc.gpsimd.tensor_copy(k_mixed[g.par][:, 1].rearrange("p t n -> p (t n)"),
                                          k_mixed[g.par][:, 0].bitcast(F32).rearrange("p t n -> p (t n)")
                                          ).then_inc(S["k_copied"], 1)

                def step(g):
                    if g.has(1):
                        self.pool_xb(pool, g + 1, [bias_o[self.L][:]] * NT)
                        k_copy(g + 1)
                    if g.has(-2):
                        self.pool_rstd(pool, g + -2)
                pipeline(pool, step)

            def tensor(self, pe):
                start_of_layer(pe, self.L)
                S = self.s
                W = {n: wt[(self.L, n)] for n in "qkvo"}

                def project_t(w, bank):
                    for ot in range(DT):
                        last = three_pass(ps[:, bank, ot * N:(ot + 1) * N],
                                          [([w[p][:, kt, ot * P:(ot + 1) * P] for p in (0, 1)],
                                            [xt[p][:, kt, :] for p in (0, 1)]) for kt in range(DT)])
                    return last

                def q(g):
                    pe.wait_ge(S["xt_high"], g.count(1, 1))
                    pe.wait_ge(S["xt_low"], g.count(1, 1))
                    wait(pe, S["v_ready"], g.count())
                    project_t(W["q"], BANK_PROJ).then_inc(S["q_ps"], 1)

                def k(g):
                    wait(pe, S["y_summed"], g.count(1, -2))
                    project_t(W["k"], BANK_PROJ + 1).then_inc(S["k_ps"], 1)

                def v(g, nt):
                    if nt == 0:
                        pe.wait_ge(S["q_low"], g.count(1, 1))
                    last = three_pass(ps[:, BANK_PROJ, nt * D:(nt + 1) * D],
                                      [([xt[p][:, kt, nt * P:(nt + 1) * P] for p in (0, 1)],
                                        [W["v"][p][:, kt, :] for p in (0, 1)]) for kt in range(DT)])
                    if nt == NT - 1:
                        last.then_inc(S["v_ps"], 1)

                def scores(g, h):
                    ot, a = divmod(h, HG)
                    if h == 0:
                        pe.wait_ge(self.qz_ready[g.par], g.turns(32 * HG, 32 * HG))
                        pe.wait_ge(self.k_mixed_ready[g.par], g.turns(16 * HG, 16 * HG))
                    wait(pe, S["max_ready"], g.count(H, h - 1))
                    for qt in range(NT):
                        for i in range(2):
                            last = nc.tensor.matmul(ps[:, BANK_S + h % 2, qt * N:(qt + 1) * N],
                                                    qz[g.par][:, a, i, ot, qt * P:(qt + 1) * P],
                                                    k_mixed[g.par][:, a % 2, ot, :], start=(i == 0), stop=(i == 1))
                    last.then_inc(S["scores_ps"], 1)

                def transpose_probs(g, h):
                    pe.wait_ge(S["exp_ready"], g.count(H, h + 1))
                    wait(pe, S["pt_odd" if h % 2 else "pt_even"], g.count(H // 2, h // 2))
                    for kt in range(NT):
                        for qt in range(NT):
                            last = nc.tensor.transpose(
                                ps[:, BANK_PT + h % 2, kt * N + qt * P:kt * N + (qt + 1) * P],
                                probs[:, h % 4, qt, kt * P:(kt + 1) * P], ident[:])
                    last.then_inc(S["pt_ps"], 1)

                def pv(g, ot):
                    if ot == 0:
                        pe.wait_ge(S["v_ready"], g.count(1, 1))
                        wait(pe, S["o_ready"], g.count())
                    pe.wait_ge(S["pt_even"], g.count(H // 2, 2 * ot + 2))
                    pe.wait_ge(S["pt_odd"], g.count(H // 2, 2 * ot + 2))
                    for kt in range(NT):
                        for a in range(HG):
                            h = ot * HG + a
                            last = nc.tensor.matmul(ps[a * DH:(a + 1) * DH, BANK_O, ot * N:(ot + 1) * N],
                                                    v_sb[:, g.par, kt, h * DH:(h + 1) * DH],
                                                    probs_t[:, h % 4, kt * N:(kt + 1) * N],
                                                    start=(kt == 0), stop=(kt == NT - 1))
                    last.then_inc(S["pv_done"], 1)

                def transpose_recip(g):
                    pe.wait_ge(S["recip_rep_ready"], g.count(1, 1))
                    wait(pe, S["recip_t_ready"], g.count())
                    if g.has(2):
                        pe.wait_ge(S["xt_low"], g.count(1, 3))
                    for ot in range(DT):
                        for qt in range(NT):
                            last = nc.tensor.transpose(
                                ps[:, BANK_X, ot * N + qt * P:ot * N + (qt + 1) * P],
                                recip_rep[:, qt, ot * P:(ot + 1) * P], ident[:])
                    last.then_inc(S["recip_t_ps"], 1)

                def project_out(g):
                    pe.wait_ge(S["o_high"], g.count(1, 1))
                    pe.wait_ge(S["o_low"], g.count(1, 1))
                    wait(pe, S["y_summed"], g.count())
                    if g.has(2):
                        pe.wait_ge(S["k_low"], g.count(1, 3))
                    for nt in range(NT):
                        last = three_pass(ps[:, BANK_PROJ + 1, nt * D:(nt + 1) * D],
                                          [([o_parts[p][:, ot, nt * P:(nt + 1) * P] for p in (0, 1)],
                                            [W["o"][p][:, ot, :] for p in (0, 1)]) for ot in range(DT)])
                    last.then_inc(S["y_ps"], 1)

                def step(g):
                    now, after, before = g.has(0), g.has(1), g.has(-1)
                    for h in range(H):
                        if now:
                            scores(g, h)
                        if h == 3 and before:
                            transpose_recip(g + -1)
                        if h == 6 and g.has(2):
                            wait(pe, S["recip_t_ready"], g.count())
                            self.pe_transpose_x(pe, g + 2)
                        if h == 2 and before:
                            pv(g + -1, 1)
                        if h == 6 and now:
                            pv(g, 0)
                        if h < 2 and before:
                            transpose_probs(g + -1, H - 2 + h)
                        if h >= 2 and now:
                            transpose_probs(g, h - 2)
                        if h == 0 and after:
                            q(g + 1)
                        if h == 1 and after:
                            k(g + 1)
                        if h in (4, 5) and after:
                            v(g + 1, h - 4)
                        if h == 7 and before:
                            project_out(g + -1)
                pipeline(pe, step)

            def scalar(self, act):
                start_of_layer(act, self.L)
                S = self.s

                def biased(dst, bank, bias, done):
                    for ot in range(DT):
                        last = nc.scalar.activation(dst[:, ot, :], ps[:, bank, ot * N:(ot + 1) * N],
                                                    ACT.Identity, bias=bias[:, ot:ot + 1])
                    last.then_inc(done, 1)

                def q_high(g):
                    act.wait_ge(S["q_ps"], g.count(1, 1))
                    p = g + -1
                    wait(act, self.qz_ready[p.par], p.turns(32 * HG, 32 * HG))
                    biased(q_parts[:, HIGH], BANK_PROJ, bias_q[self.L], S["q_high"])

                def k_high(g):
                    act.wait_ge(S["k_ps"], g.count(1, 1))
                    biased(k_mixed[g.par][:, 0], BANK_PROJ + 1, bias_k[self.L], S["k_high"])

                def v_copy(g):
                    act.wait_ge(S["v_ps"], g.count(1, 1))
                    nc.scalar.activation(v_sb[:, g.par, :, :],
                                         ps[:, BANK_PROJ, :].rearrange("p (t d) -> p t d", t=NT), ACT.Copy
                                         ).then_inc(S["v_ready"], 1)

                def exps(g, h):
                    act.wait_ge(S["max_ready"], g.count(H, h + 1))
                    for qt in range(NT):
                        j = NT * h + qt
                        last = nc.scalar.activation(probs[:, h % 4, qt, :], probs[:, h % 4, qt, :], ACT.Exp,
                                                    bias=neg_max[:, g.par, j:j + 1], scale=-1.0,
                                                    accum_out=sums[:, g.par, j:j + 1])
                    last.then_inc(S["exp_ready"], 1)

                def pt_odd(g, h):
                    act.wait_ge(S["pt_ps"], g.count(H, h + 1))
                    wait(act, S["pv_done"], g.count(2, h // HG))
                    nc.scalar.activation(probs_t[:, h % 4, :], ps[:, BANK_PT + 1, :], ACT.Copy
                                         ).then_inc(S["pt_odd"], 1)

                def recip_t_copy(g):
                    act.wait_ge(S["recip_t_ps"], g.count(1, 1))
                    wait(act, S["o_ready"], g.count())
                    nc.scalar.activation(recip_t[:].rearrange("p t n -> p (t n)"), ps[:, BANK_X, :], ACT.Copy
                                         ).then_inc(S["recip_t_ready"], 1)

                def o_high(g):
                    act.wait_ge(S["o_ready"], g.count(1, 1))
                    wait(act, S["y_ps"], g.count())
                    nc.scalar.activation(o_parts[HIGH][:], o_t[:], ACT.Copy).then_inc(S["o_high"], 1)

                def step(g):
                    now, after, before = g.has(0), g.has(1), g.has(-1)
                    for h in range(H):
                        if h == 0 and before:
                            exps(g + -1, H - 1)
                        if h >= 1 and now:
                            exps(g, h - 1)
                        if h == 1 and before:
                            pt_odd(g + -1, H - 1)
                        if h == 6 and g.has(2):
                            self.act_xt_high(act, g + 2, S["v_ps"])
                        if h in (3, 5, 7) and now:
                            pt_odd(g, h - 2)
                        if h == 1 and after:
                            q_high(g + 1)
                        if h == 3 and before:
                            recip_t_copy(g + -1)
                        if h == 5 and before:
                            o_high(g + -1)
                        if h == 2 and after:
                            k_high(g + 1)
                        if h == 5 and after:
                            v_copy(g + 1)
                pipeline(act, step)

            def vector(self, dve):
                start_of_layer(dve, self.L)
                S = self.s

                def biased_low(low, bank, bias, high, done):
                    for ot in range(DT):
                        last = nc.vector.scalar_tensor_tensor(
                            out=low[:, ot, :], in0=ps[:, bank, ot * N:(ot + 1) * N],
                            scalar=bias[:, ot:ot + 1], in1=high[:, ot, :].bitcast(F32),
                            op0=ALU.add, op1=ALU.subtract)
                    last.then_inc(done, 1)

                def q_low(g):
                    dve.wait_ge(S["q_high"], g.count(1, 1))
                    biased_low(q_parts[:, LOW], BANK_PROJ, bias_q[self.L], q_parts[:, HIGH], S["q_low"])

                def k_low(g):
                    dve.wait_ge(S["k_high"], g.count(1, 1))
                    p = g + -1
                    wait(dve, self.k_mixed_ready[p.par], p.turns(16 * HG, 16 * HG))
                    biased_low(k_low_sb, BANK_PROJ + 1, bias_k[self.L], k_mixed[g.par][:, 0], S["k_low"])

                def masked_max(g, h):
                    dve.wait_ge(S["scores_ps"], g.count(H, h + 1))
                    wait(dve, S["pt_ps"], g.count(H, h - 3))
                    part(dve)
                    for qt in range(NT):
                        j = NT * h + qt
                        last = nc.vector.tensor_tensor_reduce(
                            probs[:, h % 4, qt, :], ps[:, BANK_S + h % 2, qt * N:(qt + 1) * N],
                            mask[:, qt, :], -SCALE, HIGHEST, ALU.add, ALU.min, neg_max[:, g.par, j:j + 1])
                    last.then_inc(S["max_ready"], 1)

                def pt_even(g, h):
                    dve.wait_ge(S["pt_ps"], g.count(H, h + 1))
                    wait(dve, S["pv_done"], g.count(2, h // HG))
                    nc.vector.tensor_copy(probs_t[:, h % 4, :], ps[:, BANK_PT, :]).then_inc(S["pt_even"], 1)

                def recip_sums(g):
                    dve.wait_ge(S["exp_ready"], g.count(H, H))
                    nc.vector.reciprocal(recip[:], sums[:, g.par, :]).then_inc(S["recip_ready"], 1)
                    dve.wait_ge(S["recip_ready"], g.count(1, 1))
                    wait(dve, S["recip_t_ps"], g.count())
                    r = recip[:].rearrange("p (h q) -> p h q", q=NT)
                    for qt in range(NT):
                        last = nc.vector.tensor_scalar(recip_rep[:, qt].rearrange("p (h d) -> p h d", h=H),
                                                       r[:, :, qt:qt + 1].to_broadcast([P, H, DH]),
                                                       defined[:, qt:qt + 1], None, ALU.mult)
                    last.then_inc(S["recip_rep_ready"], 1)

                def normalize_o(g):
                    dve.wait_ge(S["pv_done"], g.count(2, 2))
                    dve.wait_ge(S["recip_t_ready"], g.count(1, 1))
                    wait(dve, S["o_low"], g.count())
                    nc.vector.tensor_tensor(o_t[:].rearrange("p t n -> p (t n)"), ps[:, BANK_O, :],
                                            recip_t[:].rearrange("p t n -> p (t n)"), ALU.mult
                                            ).then_inc(S["o_ready"], 1)

                def o_low(g):
                    dve.wait_ge(S["o_high"], g.count(1, 1))
                    nc.vector.tensor_tensor(o_parts[LOW][:].rearrange("p t n -> p (t n)"),
                                            o_t[:].rearrange("p t n -> p (t n)"),
                                            o_parts[HIGH][:].bitcast(F32).rearrange("p t n -> p (t n)"),
                                            ALU.subtract).then_inc(S["o_low"], 1)

                def y_sum(g):
                    dve.wait_ge(S["y_ps"], g.count(1, 1))
                    dve.wait_ge(S["xb_ready"], g.count(1, 1))
                    wait(dve, S["out_ready"], g.count())
                    nc.vector.tensor_tensor(y_sb[:].rearrange("p t d -> p (t d)"), ps[:, BANK_PROJ + 1, :],
                                            self.x_of(g), ALU.add).then_inc(S["y_summed"], 1)

                def step(g):
                    now, after, before = g.has(0), g.has(1), g.has(-1)
                    for h in range(H):
                        if now:
                            masked_max(g, h)
                        if h == 0 and before:
                            pt_even(g + -1, H - 2)
                        if h in (2, 4, 6) and now:
                            pt_even(g, h - 2)
                        if h == 0 and g.has(-2):
                            y_sum(g + -2)
                        if h == 1 and before:
                            recip_sums(g + -1)
                        if h == 1 and after:
                            q_low(g + 1)
                        if h == 2 and after:
                            k_low(g + 1)
                        if h == 3 and g.has(-2):
                            self.dve_stats(dve, g + -2)
                        if h == 4 and before:
                            normalize_o(g + -1)
                        if h == 5 and before:
                            o_low(g + -1)
                        if h == 5 and g.has(-2):
                            self.dve_normalize(dve, g + -2)
                        if h == 6 and g.has(2):
                            self.dve_xt_low(dve, g + 2)
                pipeline(dve, step)

        class GraphAttention(Layer):

            def __init__(self, L):
                super().__init__(L, ["dst_ps", "max_ready", "wh_ps", "e_src_ready", "wh_ready", "src_max",
                                     "row_max", "neg_max_ready", "summed", "logits_ready", "exp_ready",
                                     "pt_ps", "pt_ready", "recip_raw", "recip_ready",
                                     "neg_mean_ready", "shift_ready"])

            def sync(self, sp):
                start_of_layer(sp, self.L)

                def step(g):
                    if g.has(2):
                        self.load(sp, g + 2)
                    if g.has(-4):
                        self.store(sp, g + -4)
                pipeline(sp, step)

            def gpsimd(self, pool):
                start_of_layer(pool, self.L)

                def step(g):
                    if g.has(-2):
                        self.pool_rstd(pool, g + -2)
                        self.pool_shift(pool, g + -2)
                pipeline(pool, step)

            def tensor(self, pe):
                start_of_layer(pe, self.L)
                S = self.s

                def dst_rows(g):
                    pe.wait_ge(S["xt_high"], g.count(1, 1))
                    pe.wait_ge(S["xt_low"], g.count(1, 1))
                    wait(pe, S["max_ready"], g.count())
                    three_pass(ps[:, 1, 0:N],
                               [([dst_rep[p][:, kt, :] for p in (0, 1)], [self.xt(g)[p][:, kt, :] for p in (0, 1)])
                                for kt in range(DT)]).then_inc(S["dst_ps"], 1)

                def wh(g):
                    wait(pe, S["wh_ready"], g.count())
                    for nt in range(NT):
                        last = three_pass(ps[:, 2 + nt, 0:WE],
                                          [([self.xt(g)[p][:, kt, nt * P:(nt + 1) * P] for p in (0, 1)],
                                            [w2[p][:, kt, :] for p in (0, 1)]) for kt in range(DT)])
                    last.then_inc(S["wh_ps"], 1)

                def transpose_probs(g):
                    pe.wait_ge(S["exp_ready"], g.count(1, 1))
                    wait(pe, S["pt_ready"], g.count())
                    for mt in range(NT):
                        for nt in range(NT):
                            last = nc.tensor.transpose(ps[:, 4, mt * N + nt * P:mt * N + (nt + 1) * P],
                                                       probs[:, 2 + g.par, nt, mt * P:(mt + 1) * P], ident[:])
                    last.then_inc(S["pt_ps"], 1)

                def weighted_sum(g):
                    pe.wait_ge(S["pt_ready"], g.count(1, 1))
                    pe.wait_ge(S["wh_ready"], g.count(1, 1))
                    wait(pe, S["y_summed"], g.count(1, -1))
                    for nt in range(NT):
                        for mt in range(NT):
                            last = nc.tensor.matmul(ps[:, 6 + g.par, nt * D:(nt + 1) * D],
                                                    probs_t[:, 0, mt * N + nt * P:mt * N + (nt + 1) * P],
                                                    v_sb[:, g.par, mt, :], start=(mt == 0), stop=(mt == NT - 1))
                    last.then_inc(S["y_ps"], 1)

                def step(g):
                    if g.has(-1):
                        transpose_probs(g + -1)
                    if g.has(2):
                        self.pe_transpose_x(pe, g + 2)
                    if g.has(1):
                        dst_rows(g + 1)
                        wh(g + 1)
                    if g.has(-1):
                        weighted_sum(g + -1)
                pipeline(pe, step)

            def scalar(self, act):
                start_of_layer(act, self.L)
                S = self.s

                def wh_copy(g):
                    act.wait_ge(S["wh_ps"], g.count(1, 1))
                    wait(act, S["y_ps"], g.count(1, -1))
                    nc.scalar.activation(v_sb[:, g.par, :, :], ps[:, 2:4, 0:D], ACT.Copy
                                         ).then_inc(S["wh_ready"], 1)

                def e_src_copy(g):
                    act.wait_ge(S["wh_ps"], g.count(1, 1))
                    wait(act, S["src_max"], g.count(1, -1))
                    nc.scalar.activation(e_src[:, g.par, :], ps[:, 2:4, D], ACT.Copy
                                         ).then_inc(S["e_src_ready"], 1)

                def source_sum(g):
                    act.wait_ge(S["e_src_ready"], g.count(1, 1))
                    act.wait_ge(S["max_ready"], g.count(1, 1))
                    wait(act, S["logits_ready"], g.count())
                    for nt in range(NT):
                        last = nc.scalar.activation(probs[:, 1, nt, :], probs[:, 0, nt, :], ACT.Identity,
                                                    bias=e_src[:, g.par, nt:nt + 1])
                    last.then_inc(S["summed"], 1)

                def exps(g):
                    act.wait_ge(S["logits_ready"], g.count(1, 1))
                    act.wait_ge(S["neg_max_ready"], g.count(1, 1))
                    wait(act, S["recip_raw"], g.count(1, -1))
                    for nt in range(NT):
                        last = nc.scalar.activation(probs[:, 2 + g.par, nt, :], probs[:, 2 + g.par, nt, :],
                                                    ACT.Exp, bias=node_max[:, 2, nt:nt + 1],
                                                    accum_out=sums[:, g.par, nt:nt + 1])
                    last.then_inc(S["exp_ready"], 1)

                def step(g):
                    if g.has(0):
                        wh_copy(g)
                    if g.has(2):
                        self.act_xt_high(act, g + 2, S["wh_ps"])
                    if g.has(0):
                        exps(g)
                    if g.has(-3):
                        self.act_normalize(act, g + -3)
                    if g.has(1):
                        e_src_copy(g + 1)
                        source_sum(g + 1)
                pipeline(act, step)

            def vector(self, dve):
                start_of_layer(dve, self.L)
                S = self.s

                def masked_max(g):
                    dve.wait_ge(S["dst_ps"], g.count(1, 1))
                    wait(dve, S["summed"], g.count())
                    part(dve)
                    for nt in range(NT):
                        last = nc.vector.tensor_tensor_reduce(probs[:, 0, nt, :], ps[:, 1, 0:N], mask[:, nt, :],
                                                              1.0, LOWEST, ALU.add, ALU.max,
                                                              maxes[:, g.par, nt:nt + 1])
                    last.then_inc(S["max_ready"], 1)

                def pt_copy(g):
                    dve.wait_ge(S["pt_ps"], g.count(1, 1))
                    wait(dve, S["y_ps"], g.count())
                    nc.vector.tensor_scalar(probs_t[:, 0, :], ps[:, 4, :], 0.0, None, ALU.max
                                            ).then_inc(S["pt_ready"], 1)

                def raw_recip(g):
                    dve.wait_ge(S["exp_ready"], g.count(1, 1))
                    nc.vector.reciprocal(src_recip[:, 0, :], sums[:, g.par, :NT]).then_inc(S["recip_raw"], 1)

                def guarded_recip(g):
                    dve.wait_ge(S["recip_raw"], g.count(1, 1))
                    nc.vector.scalar_tensor_tensor(out=src_recip[:, 1, :], in0=src_recip[:, 0, :], scalar=0.0,
                                                   in1=row_any[:], op0=ALU.max, op1=ALU.mult
                                                   ).then_inc(S["recip_ready"], 1)

                def source_max(g):
                    dve.wait_ge(S["e_src_ready"], g.count(1, 1))
                    dve.wait_ge(S["max_ready"], g.count(1, 1))
                    nc.vector.tensor_tensor(node_max[:, 0, :], maxes[:, g.par, 0:NT], e_src[:, g.par, :], ALU.add
                                            ).then_inc(S["src_max"], 1)

                def row_max(g):
                    dve.wait_ge(S["src_max"], g.count(1, 1))
                    nc.vector.scalar_tensor_tensor(out=node_max[:, 1, :], in0=node_max[:, 0, :], scalar=NEG_SLOPE,
                                                   in1=node_max[:, 0, :], op0=ALU.mult, op1=ALU.max
                                                   ).then_inc(S["row_max"], 1)

                def negated_max(g):
                    dve.wait_ge(S["row_max"], g.count(1, 1))
                    wait(dve, S["exp_ready"], g.count())
                    nc.vector.tensor_scalar(node_max[:, 2, :], node_max[:, 1, :], -1.0, None, ALU.mult
                                            ).then_inc(S["neg_max_ready"], 1)

                def leaky(g):
                    dve.wait_ge(S["summed"], g.count(1, 1))
                    wait(dve, S["pt_ps"], g.count(1, -1))
                    nc.vector.scalar_tensor_tensor(out=probs[:, 2 + g.par].rearrange("p t n -> p (t n)"),
                                                   in0=probs[:, 1].rearrange("p t n -> p (t n)"),
                                                   scalar=NEG_SLOPE,
                                                   in1=probs[:, 1].rearrange("p t n -> p (t n)"),
                                                   op0=ALU.mult, op1=ALU.max).then_inc(S["logits_ready"], 1)

                def y_sum(g):
                    dve.wait_ge(S["y_ps"], g.count(1, 1))
                    dve.wait_ge(S["recip_ready"], g.count(1, 1))
                    wait(dve, S["out_ready"], g.count(1, -1))
                    for nt in range(NT):
                        last = nc.vector.scalar_tensor_tensor(
                            out=self.y(g)[:, nt, :], in0=ps[:, 6 + g.par, nt * D:(nt + 1) * D],
                            scalar=src_recip[:, 1, nt:nt + 1], in1=self.x_of(g, slice(nt, nt + 1)),
                            op0=ALU.mult, op1=ALU.add)
                    last.then_inc(S["y_summed"], 1)

                def step(g):
                    if g.has(0):
                        source_max(g)
                    if g.has(-2):
                        y_sum(g + -2)
                    if g.has(0):
                        row_max(g)
                        leaky(g)
                        negated_max(g)
                    if g.has(-1):
                        pt_copy(g + -1)
                        raw_recip(g + -1)
                    if g.has(2):
                        self.dve_xt_low(dve, g + 2)
                    if g.has(1):
                        masked_max(g + 1)
                    if g.has(-1):
                        guarded_recip(g + -1)
                    if g.has(-2):
                        self.dve_stats(dve, g + -2)
                pipeline(dve, step)

        layers = [MessagePassing(0), Attention(1), GraphAttention(2), Attention(3)]

        block = ctx.enter_context(nc.Block())

        @block.sync
        def _(sp):
            prep_sync(sp)
            for layer in layers:
                layer.sync(sp)
            sp.wait_ge(layer_done[3][0], 16 * (B // 2))
            sp.wait_ge(layer_done[3][1], 16 * (B // 2))

        @block.gpsimd
        def _(pool):
            prep_gpsimd(pool)
            for layer in layers:
                layer.gpsimd(pool)

        @block.tensor
        def _(pe):
            prep_tensor(pe)
            for layer in layers:
                layer.tensor(pe)

        @block.scalar
        def _(act):
            prep_scalar(act)
            for layer in layers:
                layer.scalar(act)

        @block.vector
        def _(dve):
            prep_vector(dve)
            for layer in layers:
                layer.vector(dve)


_INS = ["x", "adj", "L0_gnn_W", "L0_gnn_b", "L1_gnn_Wq", "L1_gnn_bq", "L1_gnn_Wk", "L1_gnn_bk", "L1_gnn_Wv",
        "L1_gnn_bv", "L1_gnn_Wo", "L1_gnn_bo", "L2_gnn_W", "L2_gnn_a_src", "L2_gnn_a_dst", "L3_gnn_Wq",
        "L3_gnn_bq", "L3_gnn_Wk", "L3_gnn_bk", "L3_gnn_Wv", "L3_gnn_bv", "L3_gnn_Wo", "L3_gnn_bo"]


def kernel(**inputs):
    import numpy as _np
    import concourse.bacc as _bacc
    from concourse import mybir as _mybir
    from concourse.bass_utils import run_bass_kernel_spmd as _run

    nc = _bacc.Bacc("TRN2", target_bir_lowering=False, num_devices=1)
    arrays, args = {}, []
    for name in _INS:
        a = _np.ascontiguousarray(inputs[name])
        arrays[f"in_{name}"] = a
        args.append(nc.dram_tensor(f"in_{name}", a.shape, _mybir.dt.from_np(a.dtype), kind="ExternalInput").ap())
    args.append(nc.dram_tensor("out_y", (B, N, D), _mybir.dt.float32, kind="ExternalOutput").ap())
    graph_layers_kernel(nc, *args)
    r = _run(nc, [arrays], core_ids=[0])
    return r.results[0]["out_y"]
```

```python
import concourse.bass as bass
from concourse import mybir
from contextlib import ExitStack

F32 = mybir.dt.float32
F32R = mybir.dt.float32r
I32 = mybir.dt.int32
ACT = mybir.ActivationFunctionType
ALU = mybir.AluOpType
AX = mybir.AxisListType

P = 128
B, N, D = 32, 256, 256
NT = N // P
DT = D // P
H = 8
DH = D // H
HG = P // DH
SCALE = DH ** -0.5
EPS = 1e-5
NEG_SLOPE = 0.2
MASKED = -1.0e38
LOWEST, HIGHEST = -3.0e38, 3.0e38
WE = D + 2
HIGH, LOW = 0, 1


class Graph:

    def __init__(self, t, par):
        self.t, self.par = t, par

    def __add__(self, n):
        k = self.par + n
        return Graph(self.t + k // 2, k % 2)

    def has(self, n):
        return not isinstance(self.t, int) or 0 <= 2 * self.t + self.par + n < B

    def is_number(self, n):
        return isinstance(self.t, int) and 2 * self.t + self.par == n

    def count(self, k=1, c=0):
        return self.t * (2 * k) + (self.par * k + c)

    def turns(self, k=1, c=0):
        return self.t * k + c


def wait(eng, sem, value):
    if not isinstance(value, int) or value > 0:
        eng.wait_ge(sem, value)


HEAD = 6


def run_layers(eng, steps, opening, start, opened_after):
    for L, step in enumerate(steps):
        if L == 0:
            step(Graph(-1, 0))
            step(Graph(-1, 1))
        start(eng, L)
        for n in range(HEAD):
            step(Graph(n // 2, n % 2))
        with eng.Fori(0, (B - HEAD - 2) // 2) as t:
            step(Graph(t + HEAD // 2, 0))
            step(Graph(t + HEAD // 2, 1))
        for n in range(B - 2, B + 4):
            step(Graph(n // 2, n % 2))
            for opens in opened_after.get((L, n), ()):
                if opens == -2:
                    opening(eng, L + 1)
                steps[L + 1](Graph(-1, opens + 2))


OPENED_AFTER = {(0, B - 1): [-2], (0, B): [-1], (1, B): [-2, -1], (2, B - 1): [-2], (2, B): [-1]}
TRANSFERS_OPENED_AFTER = {**OPENED_AFTER, (2, B): [], (2, B + 1): [-1]}


def graph_layers_kernel(nc, x, adj, L0_W, L0_b, L1_Wq, L1_bq, L1_Wk, L1_bk, L1_Wv, L1_bv, L1_Wo, L1_bo,
                        L2_W, L2_a_src, L2_a_dst,
                        L3_Wq, L3_bq, L3_Wk, L3_bk, L3_Wv, L3_bv, L3_Wo, L3_bo, out):
    ctx = ExitStack()
    with ctx:
        def sb(name, shape, dt=F32):
            return ctx.enter_context(nc.sbuf_tensor(name, shape, dt))

        def sem(name):
            return ctx.enter_context(nc.semaphore(name))

        x_res = sb("x_res", [P, B, NT * D])
        ident = sb("ident", [P, P])
        mask = sb("mask", [P, NT, N])
        row_any = sb("row_any", [P, NT])
        defined = sb("defined", [P, NT])
        deg = sb("deg", [P, NT])
        w0 = [sb(f"w0_{p}", [P, DT, 2 * D], F32R) for p in "hl"]
        wt = {(L, n): [sb(f"w{L}{n}_{p}", [P, DT, D], F32R) for p in "hl"] for L in (1, 3) for n in "qkvo"}
        w2 = [sb(f"w2_{p}", [P, DT, WE], F32R) for p in "hl"]
        dst_rep = [sb(f"dst_rep_{p}", [P, DT, P], F32R) for p in "hl"]
        bias_q = {L: sb(f"bias_q{L}", [P, DT]) for L in (1, 3)}
        bias_k = {L: sb(f"bias_k{L}", [P, DT]) for L in (1, 3)}
        bias_v = {L: sb(f"bias_v{L}", [P, DT]) for L in (1, 3)}
        bias_o = {L: sb(f"bias_o{L}", [P, D]) for L in (1, 3)}

        x_in = sb("x_in", [P, 2, NT * D])
        xt = [sb(f"xt_{p}", [P, DT, N], F32R) for p in "hl"]
        q_parts = sb("q_parts", [P, 2, DT, N], F32R)
        k_mixed = [sb(f"k_mixed{i}", [P, 2, DT, N], F32R) for i in range(2)]
        k_low_sb = sb("k_low_sb", [P, DT, N], F32R)
        qz = [sb(f"qz{i}", [P, HG, 2, DT, N], F32R) for i in range(2)]
        v_sb = sb("v_sb", [P, 2, NT, D])
        probs = sb("probs", [P, 4, NT, N])
        probs_t = sb("probs_t", [P, 4, NT * N])
        maxes = sb("maxes", [P, 2, NT])
        neg_max = sb("neg_max", [P, 2, 2 * H])
        sums = sb("sums", [P, 2, 2 * H])
        recip = sb("recip", [P, 2 * H])
        recip_rep = sb("recip_rep", [P, NT, D])
        recip_t = sb("recip_t", [P, DT, N])
        o_t = sb("o_t", [P, DT, N])
        o_parts = [sb(f"o_t_{p}", [P, DT, N], F32R) for p in "hl"]
        y_sb = sb("y_sb", [P, NT, D])
        y_out = sb("y_out", [P, 2, NT * D])
        node_max = sb("node_max", [P, 3, NT])
        e_src = sb("e_src", [P, 2, NT])
        neg_mean = sb("neg_mean", [P, NT])
        shift = sb("shift", [P, NT])
        src_recip = sb("src_recip", [P, 2, NT])
        stats = sb("stats", [P, NT, 6])
        mean_var = sb("mean_var", [P, NT, 2])
        var_eps = sb("var_eps", [P, NT])
        rstd = sb("rstd", [P, NT])
        minus_half = sb("minus_half", [P, NT])

        adj_t = [o_parts[p][:] for p in (HIGH, LOW)]
        mj_high, mj_low = k_mixed[1], q_parts
        deg_b = o_t
        y_pair = probs_t[:, 2:4, :].rearrange("p a (t d) -> p a t d", t=NT)

        ps = ctx.enter_context(nc.psum_tensor("ps", [P, 8, 512], F32))
        BANK_X, BANK_O, BANK_PROJ, BANK_S, BANK_PT = 0, 1, 2, 4, 6

        raw_names = ["0i", "0j", "1q", "1k", "1v", "1o", "3q", "3k", "3v", "3o"]
        raw_src = {"0i": L0_W[:, 0:D], "0j": L0_W[:, D:2 * D], "1q": L1_Wq, "1k": L1_Wk, "1v": L1_Wv,
                   "1o": L1_Wo, "3q": L3_Wq, "3k": L3_Wk, "3v": L3_Wv, "3o": L3_Wo}
        raw = {n: x_res[:, i, :].rearrange("p (t d) -> p t d", t=DT) for i, n in enumerate(raw_names)}
        raw2 = x_res[:, 10, :].rearrange("p (t d) -> p t d", t=DT)
        adj_i = x_res[:, 11, :].rearrange("p (t d) -> p t d", t=NT).bitcast(I32)
        adj_f = x_res[:, 20, :].rearrange("p (t n) -> p t n", t=NT)
        rows = {n: x_res[:, 12 + i, 0:D] for i, n in enumerate(["b0", "bo1", "bo3", "asrc", "adst"])}
        zeros = x_res[:, 17, 0:P]
        scratch = x_res[:, 18, 0:D]
        va = x_res[:, 19, 0:4]
        bv_rep = {L: [xt[p][:, :, 0:P] if L == 1 else xt[p][:, :, P:2 * P] for p in (0, 1)]
                  for L in (1, 3)}
        row_src = {"b0": L0_b, "bo1": L1_bo, "bo3": L3_bo, "asrc": L2_a_src, "adst": L2_a_dst}

        def weight_dst(n, p):
            if n == "0i":
                return w0[p][:, :, 0:D]
            if n == "0j":
                return w0[p][:, :, D:2 * D]
            return wt[(int(n[0]), n[1])][p][:, :, :]

        adj_loaded = sem("adj_loaded")
        weight_loaded = {n: sem(f"weight_loaded_{n}") for n in ("0i", "0j", "1", "2", "3")}

        def loaded(n):
            return (weight_loaded[n], 16) if n in weight_loaded else (weight_loaded[n[0]], 64)
        rows_loaded = sem("rows_loaded")
        ident_ready = sem("ident_ready")
        consts_ready = sem("consts_ready")
        wt_transposed = sem("wt_transposed")
        wt_high = sem("wt_high")
        wt_low = sem("wt_low")
        prep_step = sem("prep_step")
        va_ready = sem("va_ready")
        column_high = sem("column_high")
        column_low = sem("column_low")
        bias_product = sem("bias_product")
        qz_zeroed = sem("qz_zeroed")
        prepared = sem("prepared")
        apart = sem("apart")
        layer_done = [[sem(f"layer{L}_stored{p}") for p in range(2)] for L in range(4)]

        def start_of_layer(eng, L):
            if L == 0:
                eng.wait_ge(prepared, 2)
            else:
                eng.wait_ge(layer_done[L - 1][0], 16 * (B // 2))
                eng.wait_ge(layer_done[L - 1][1], 16 * (B // 2))

        def part(eng):
            eng.sem_inc(apart, 1)

        def three_pass(pe_out, pairs):
            n = len(pairs) * 3
            i = 0
            for st, mv in pairs:
                for a, b in ((HIGH, HIGH), (HIGH, LOW), (LOW, HIGH)):
                    last = nc.tensor.matmul(pe_out, st[a], mv[b], start=(i == 0), stop=(i == n - 1))
                    i += 1
            return last

        N_RAW = len(raw_names)

        def prep_sync(sp):
            sp.dma_start(raw["0i"], raw_src["0i"].rearrange("(t p) d -> p t d", p=P)).then_inc(loaded("0i")[0], 16)
            sp.dma_start(adj_i, adj.rearrange("(t p) d -> p t d", p=P)).then_inc(adj_loaded, 16)
            for n in raw_names[1:]:
                sp.dma_start(raw[n], raw_src[n].rearrange("(t p) d -> p t d", p=P)).then_inc(loaded(n)[0], 16)
            sp.dma_start(raw2, L2_W.rearrange("(t p) d -> p t d", p=P)).then_inc(weight_loaded["2"], 16)
            for n, src in row_src.items():
                sp.dma_start(rows[n], src.partition_broadcast(P)).then_inc(rows_loaded, 16)
            for dst, src in ((bias_q[1], L1_bq), (bias_k[1], L1_bk), (bias_v[1], L1_bv),
                             (bias_q[3], L3_bq), (bias_k[3], L3_bk), (bias_v[3], L3_bv)):
                sp.dma_start(dst[:], src.rearrange("(t p) -> p t", p=P), allow_slow_non_contiguous=True).then_inc(rows_loaded, 16)

        columns = [(bv_rep[L][HIGH][:, dt, :], bv_rep[L][LOW][:, dt, :], bias_v[L][:, dt:dt + 1], P)
                   for L in (1, 3) for dt in range(DT)]
        N_BV = len(columns)
        for dt in range(DT):
            columns.append((w2[HIGH][:, dt, D:WE], w2[LOW][:, dt, D:WE], va[:, dt:dt + 1], WE - D))
            columns.append((dst_rep[HIGH][:, dt, :], dst_rep[LOW][:, dt, :], va[:, 2 + dt:3 + dt], P))

        def prep_gpsimd(pool):
            nc.gpsimd.memset(ident[:], 0.0).then_inc(ident_ready, 1)
            pool.wait_ge(ident_ready, 1)
            nc.gpsimd.affine_select(out=ident[:], in_=ident[:], compare_op=ALU.not_equal, fill=1.0, base=0,
                                    pattern=[[-1, P]], channel_multiplier=1).then_inc(ident_ready, 1)
            nc.gpsimd.memset(zeros, 0.0).then_inc(consts_ready, 1)
            nc.gpsimd.memset(minus_half[:], -0.5).then_inc(consts_ready, 1)
            for i in range(2):
                nc.gpsimd.memset(qz[i][:].bitcast(F32).rearrange("p a b c d -> p (a b c d)"), 0.0).then_inc(qz_zeroed, 1)
            for i, (high, low, col, n) in enumerate(columns):
                pool.wait_ge(column_high, i + 1)
                nc.gpsimd.tensor_scalar(low, high.bitcast(F32), col, -1.0, ALU.subtract, ALU.mult
                                        ).then_inc(column_low, 1)
            pool.wait_ge(column_low, len(columns))
            pool.sem_inc(prepared, 1)
            pool.wait_ge(prepared, 2)

        def prep_tensor(pe):
            pe.wait_ge(ident_ready, 2)
            for i, n in enumerate(raw_names):
                pe.wait_ge(*loaded(n))
                wait(pe, wt_low, i - 3)
                for dt in range(DT):
                    for ot in range(DT):
                        last = nc.tensor.transpose(ps[:, i % 4, dt * D + ot * P:dt * D + (ot + 1) * P],
                                                   raw[n][:, ot, dt * P:(dt + 1) * P], ident[:])
                last.then_inc(wt_transposed, 1)
            pe.wait_ge(prep_step, 1)
            for jt in range(NT):
                for it in range(NT):
                    last = nc.tensor.transpose(ps[:, 4, jt * N + it * P:jt * N + (it + 1) * P],
                                               adj_f[:, it, jt * P:(jt + 1) * P], ident[:])
            last.then_inc(wt_transposed, 1)
            pe.wait_ge(wt_low, N_RAW)
            pe.wait_ge(column_low, 4)
            for L in (1, 3):
                last = three_pass(ps[:, 5 + L // 2, 0:D],
                                  [([bv_rep[L][p][:, ct, :] for p in (0, 1)],
                                    [wt[(L, "o")][p][:, ct, :] for p in (0, 1)]) for ct in range(DT)])
            last.then_inc(bias_product, 1)

        def prep_scalar(act):
            for i, n in enumerate(raw_names):
                act.wait_ge(wt_transposed, i + 1)
                nc.scalar.activation(weight_dst(n, HIGH), ps[:, i % 4, :].rearrange("p (t d) -> p t d", t=DT),
                                     ACT.Copy).then_inc(wt_high, 1)
            act.wait_ge(consts_ready, 2)
            act.wait_ge(rows_loaded, 16 * 11)
            for i, (high, low, col, n) in enumerate(columns):
                if i == N_BV:
                    act.wait_ge(va_ready, 1)
                nc.scalar.activation(high, zeros[:, 0:n], ACT.Identity, bias=col).then_inc(column_high, 1)

        def prep_vector(dve):
            done = [0]

            def link(ins):
                done[0] += 1
                ins.then_inc(prep_step, 1)
                dve.wait_ge(prep_step, done[0])

            dve.wait_ge(adj_loaded, 16)
            link(nc.vector.tensor_copy(adj_f, adj_i))
            for i, n in enumerate(raw_names):
                dve.wait_ge(wt_high, i + 1)
                nc.vector.tensor_tensor(weight_dst(n, LOW), ps[:, i % 4, :].rearrange("p (t d) -> p t d", t=DT),
                                        weight_dst(n, HIGH).bitcast(F32), ALU.subtract).then_inc(wt_low, 1)
            link(nc.vector.reduce_sum(deg[:], adj_f, AX.X))
            link(nc.vector.tensor_scalar(mask[:], adj_f, 0.0, MASKED, ALU.is_equal, ALU.mult))
            link(nc.vector.reduce_max(row_any[:], mask[:], AX.X))
            link(nc.vector.tensor_scalar(row_any[:], row_any[:], 0.0, None, ALU.is_equal))
            link(nc.vector.reciprocal(defined[:], row_any[:]))
            link(nc.vector.tensor_tensor(defined[:], defined[:], row_any[:], ALU.mult))
            dve.wait_ge(wt_transposed, N_RAW + 1)
            link(nc.vector.tensor_copy(adj_t[HIGH].rearrange("p t n -> p (t n)"), ps[:, 4, :]))
            link(nc.vector.tensor_tensor(adj_t[LOW].rearrange("p t n -> p (t n)"), ps[:, 4, :],
                                         adj_t[HIGH].bitcast(F32).rearrange("p t n -> p (t n)"), ALU.subtract))
            dve.wait_ge(rows_loaded, 16 * 11)
            for nt in range(NT):
                link(nc.vector.tensor_scalar(deg_b[:, nt, :], rows["b0"], deg[:, nt:nt + 1], None, ALU.mult))
            dve.wait_ge(weight_loaded["2"], 16)
            for i, row in enumerate(("asrc", "adst")):
                for dt in range(DT):
                    link(nc.vector.tensor_tensor_reduce(scratch, raw2[:, dt, :], rows[row], 1.0, 0.0,
                                                        ALU.mult, ALU.add, va[:, 2 * i + dt:2 * i + dt + 1]))
            dve.sem_inc(va_ready, 1)
            link(nc.vector.tensor_copy(w2[HIGH][:, :, 0:D], raw2))
            link(nc.vector.tensor_tensor(w2[LOW][:, :, 0:D], raw2, w2[HIGH][:, :, 0:D].bitcast(F32), ALU.subtract))

            dve.wait_ge(bias_product, 1)
            link(nc.vector.tensor_tensor(bias_o[1][:], ps[:, 5, 0:D], rows["bo1"], ALU.add))
            nc.vector.tensor_tensor(bias_o[3][:], ps[:, 6, 0:D], rows["bo3"], ALU.add).then_inc(prepared, 1)

        class Layer:

            def __init__(self, L, names):
                self.L = L
                if L != 2:
                    names = names + ["residual_ready"]
                shared = ["xt_ps", "xt_high", "xt_low", "y_ps", "y_summed", "y_stats", "y_var",
                          "var_eps_ready", "rstd_ready", "out_ready"]
                self.s = {n: sem(f"L{L}_{n}") for n in shared + names}
                self.x_loaded = [sem(f"L{L}_x_loaded{p}") for p in range(2)]
                self.stored = layer_done[L]

            def load(self, sp, g):
                wait(sp, self.s["xt_ps"], g.count(1, -1))
                if self.L != 2:
                    wait(sp, self.s["residual_ready"], g.count(1, -1))
                dst = x_in[:, g.par, :]
                if self.L == 0:
                    sp.dma_start(dst.rearrange("p (t d) -> p t d", t=NT),
                                 x.rearrange("b (t p) d -> p (b t) d", p=P)[:, bass.ds(g.count(NT), NT), :]
                                 ).then_inc(self.x_loaded[g.par], 16)
                else:
                    sp.dma_start(dst, x_res[:, bass.ds(g.count(), 1), :].rearrange("p a n -> p (a n)")
                                 ).then_inc(self.x_loaded[g.par], 16)

            def store(self, sp, g):
                sp.wait_ge(self.s["out_ready"], g.count(1, 1))
                src = y_out[:, g.par, :]
                if self.L == 3:
                    sp.dma_start(out.rearrange("b (t p) d -> p (b t) d", p=P)[:, bass.ds(g.count(NT), NT), :],
                                 src.rearrange("p (t d) -> p t d", t=NT)).then_inc(self.stored[g.par], 16)
                else:
                    sp.dma_start(x_res[:, bass.ds(g.count(), 1), :].rearrange("p a n -> p (a n)"), src
                                 ).then_inc(self.stored[g.par], 16)

            def pe_transpose_x(self, pe, g):
                pe.wait_ge(self.x_loaded[g.par], g.turns(16, 16))
                wait(pe, self.s["xt_low"], g.count())
                for dt in range(DT):
                    for nt in range(NT):
                        last = nc.tensor.transpose(
                            ps[:, BANK_X, dt * N + nt * P:dt * N + (nt + 1) * P],
                            x_in[:, g.par, nt * D + dt * P:nt * D + (dt + 1) * P], ident[:])
                last.then_inc(self.s["xt_ps"], 1)

            def act_xt_high(self, act, g, xt_used):
                act.wait_ge(self.s["xt_ps"], g.count(1, 1))
                wait(act, xt_used, g.count(1, 0 if self.L in (1, 3) else -1))
                nc.scalar.activation(self.xt(g)[HIGH].rearrange("p t n -> p (t n)"), ps[:, BANK_X, :], ACT.Copy
                                     ).then_inc(self.s["xt_high"], 1)

            def dve_xt_low(self, dve, g):
                dve.wait_ge(self.s["xt_high"], g.count(1, 1))
                nc.vector.tensor_tensor(self.xt(g)[LOW].rearrange("p t n -> p (t n)"), ps[:, BANK_X, :],
                                        self.xt(g)[HIGH].bitcast(F32).rearrange("p t n -> p (t n)"),
                                        ALU.subtract).then_inc(self.s["xt_low"], 1)

            def xt(self, g):
                if self.L in (1, 3) or g.par == 0:
                    return [xt[HIGH][:], xt[LOW][:]]
                return [k_mixed[0][:, HIGH], k_mixed[0][:, LOW]]

            def y(self, g):
                return y_pair[:, g.par] if self.L in (0, 2) else y_sb

            def dve_stats(self, dve, g):
                dve.wait_ge(self.s["y_summed"], g.count(1, 1))
                for nt in range(NT):
                    last = nc.vector.bn_stats(stats[:, nt, :], self.y(g)[:, nt, :])
                last.then_inc(self.s["y_stats"], 1)
                dve.wait_ge(self.s["y_stats"], g.count(1, 1))
                wait(dve, self.s["rstd_ready"], g.count())
                if self.L in (0, 2):
                    wait(dve, self.s["shift_ready"], g.count())
                part(dve)
                for nt in range(NT):
                    last = nc.vector.bn_aggr(mean_var[:, nt, :], stats[:, nt, :])
                last.then_inc(self.s["y_var"], 1)

            def pool_rstd(self, pool, g):
                pool.wait_ge(self.s["y_var"], g.count(1, 1))
                part(pool)
                nc.gpsimd.tensor_scalar(var_eps[:], mean_var[:, :, 1], EPS, 1.0, ALU.add, ALU.mult
                                        ).then_inc(self.s["var_eps_ready"], 1)
                pool.wait_ge(self.s["var_eps_ready"], g.count(1, 1))
                wait(pool, self.s["out_ready"], g.count())
                nc.gpsimd.tensor_tensor(rstd[:], var_eps[:], minus_half[:], ALU.pow
                                        ).then_inc(self.s["rstd_ready"], 1)

            def dve_normalize(self, dve, g):
                dve.wait_ge(self.s["rstd_ready"], g.count(1, 1))
                wait(dve, self.stored[g.par], g.turns(16))
                for nt in range(NT):
                    last = nc.vector.tensor_scalar(y_out[:, g.par, nt * D:(nt + 1) * D], self.y(g)[:, nt, :],
                                                   mean_var[:, nt, 0:1], rstd[:, nt:nt + 1],
                                                   ALU.subtract, ALU.mult)
                last.then_inc(self.s["out_ready"], 1)

            def pool_shift(self, pool, g):
                nc.gpsimd.tensor_scalar(neg_mean[:], mean_var[:, :, 0], -1.0, 1.0, ALU.mult, ALU.mult
                                        ).then_inc(self.s["neg_mean_ready"], 1)
                pool.wait_ge(self.s["neg_mean_ready"], g.count(1, 1))
                pool.wait_ge(self.s["rstd_ready"], g.count(1, 1))
                nc.gpsimd.tensor_tensor(shift[:], neg_mean[:], rstd[:], ALU.mult
                                        ).then_inc(self.s["shift_ready"], 1)

            def act_normalize(self, act, g):
                act.wait_ge(self.s["shift_ready"], g.count(1, 1))
                wait(act, self.stored[g.par], g.turns(16))
                for nt in range(NT):
                    last = nc.scalar.activation(y_out[:, g.par, nt * D:(nt + 1) * D], self.y(g)[:, nt, :],
                                                ACT.Identity, bias=shift[:, nt:nt + 1], scale=rstd[:, nt:nt + 1])
                last.then_inc(self.s["out_ready"], 1)

            def x_of(self, g, tiles=slice(0, NT)):
                return x_res[:, bass.ds(g.count(), 1), tiles.start * D:tiles.stop * D].rearrange("p a n -> p (a n)")

            def pool_residual(self, pool, g, const):
                pool.wait_ge(self.x_loaded[g.par], g.turns(16, 16))
                part(pool)
                for nt in range(NT):
                    s = slice(nt * D, (nt + 1) * D)
                    last = nc.gpsimd.tensor_tensor(self.x_of(g, slice(nt, nt + 1)), x_in[:, g.par, s], const[nt],
                                                   ALU.add)
                last.then_inc(self.s["residual_ready"], 1)

        class MessagePassing(Layer):
            def __init__(self, L):
                super().__init__(L, ["m_ps", "mj_high_ready", "mj_low_ready", "mi_scaled",
                                     "neg_mean_ready", "shift_ready"])

            def sync(self, sp):
                def step(g):
                    if g.has(2):
                        self.load(sp, g + 2)
                    if g.has(-3):
                        self.store(sp, g + -3)
                return step

            def gpsimd(self, pool):
                def step(g):
                    if g.has(1):
                        self.pool_residual(pool, g + 1, [deg_b[:, nt, :] for nt in range(NT)])
                    if g.has(-2):
                        self.pool_rstd(pool, g + -2)
                        self.pool_shift(pool, g + -2)
                return step

            def tensor(self, pe):
                S = self.s

                def products(g):
                    pe.wait_ge(S["xt_high"], g.count(1, 1))
                    pe.wait_ge(S["xt_low"], g.count(1, 1))
                    wait(pe, S["mi_scaled"], g.count(1, -1))
                    for nt in range(NT):
                        last = three_pass(ps[:, 2 + 2 * g.par + nt, :],
                                          [([self.xt(g)[p][:, kt, nt * P:(nt + 1) * P] for p in (0, 1)],
                                            [w0[p][:, kt, :] for p in (0, 1)]) for kt in range(DT)])
                    last.then_inc(S["m_ps"], 1)

                def mix(g):
                    pe.wait_ge(S["mj_low_ready"], g.count(1, 1))
                    wait(pe, S["y_summed"], g.count(1, -1))
                    mj = [mj_high[:, g.par], mj_low[:, g.par]]
                    for it in range(NT):
                        last = three_pass(ps[:, 6 + g.par, it * D:(it + 1) * D],
                                          [([adj_t[p][:, jt, it * P:(it + 1) * P] for p in (0, 1)],
                                            [mj[p][:, jt, :] for p in (0, 1)]) for jt in range(NT)])
                    last.then_inc(S["y_ps"], 1)

                def step(g):
                    if g.has(1):
                        self.pe_transpose_x(pe, g + 1)
                    if g.has(0):
                        products(g)
                    if g.has(-1):
                        mix(g + -1)
                return step

            def scalar(self, act):
                S = self.s

                def step(g):
                    if g.has(1):
                        self.act_xt_high(act, g + 1, S["m_ps"])
                    if g.has(-3):
                        self.act_normalize(act, g + -3)
                    if g.has(0):
                        act.wait_ge(S["m_ps"], g.count(1, 1))
                        wait(act, S["y_ps"], g.count(1, -1))
                        nc.scalar.activation(mj_high[:, g.par],
                                             ps[:, 2 + 2 * g.par:4 + 2 * g.par, D:2 * D], ACT.Copy
                                             ).then_inc(S["mj_high_ready"], 1)
                return step

            def vector(self, dve):
                S = self.s

                def split_mj(g):
                    dve.wait_ge(S["mj_high_ready"], g.count(1, 1))
                    nc.vector.tensor_tensor(mj_low[:, g.par], ps[:, 2 + 2 * g.par:4 + 2 * g.par, D:2 * D],
                                            mj_high[:, g.par].bitcast(F32), ALU.subtract).then_inc(S["mj_low_ready"], 1)

                def scale_mi(g):
                    dve.wait_ge(S["residual_ready"], g.count(1, 1))
                    for nt in range(NT):
                        last = nc.vector.scalar_tensor_tensor(
                            out=probs[:, g.par, nt, :], in0=ps[:, 2 + 2 * g.par + nt, 0:D],
                            scalar=deg[:, nt:nt + 1], in1=self.x_of(g, slice(nt, nt + 1)),
                            op0=ALU.mult, op1=ALU.add)
                    last.then_inc(S["mi_scaled"], 1)

                def y_sum(g):
                    dve.wait_ge(S["y_ps"], g.count(1, 1))
                    dve.wait_ge(S["mi_scaled"], g.count(1, 1))
                    wait(dve, S["out_ready"], g.count(1, -1))
                    nc.vector.tensor_tensor(self.y(g).rearrange("p t d -> p (t d)"), ps[:, 6 + g.par, :],
                                            probs[:, g.par, :, :].rearrange("p t d -> p (t d)"), ALU.add
                                            ).then_inc(S["y_summed"], 1)

                def step(g):
                    if g.has(1):
                        self.dve_xt_low(dve, g + 1)
                    if g.has(-2):
                        y_sum(g + -2)
                        self.dve_stats(dve, g + -2)
                    if g.has(0):
                        split_mj(g)
                        scale_mi(g)
                return step

        class Attention(Layer):

            def __init__(self, L):
                super().__init__(L, ["q_ps", "k_ps", "v_ps", "q_high", "q_low", "k_high", "k_copied", "k_low", "v_ready",
                                     "scores_ps", "max_ready", "exp_ready",
                                     "pt_ps",
                                     "pt_even", "pt_odd",
                                     "pv_done",
                                     "recip_ready", "recip_rep_ready", "recip_t_ps", "recip_t_ready",
                                     "o_ready", "o_high", "o_low"])
                self.qz_ready = [sem(f"L{L}_qz_ready{p}") for p in range(2)]
                self.k_mixed_ready = [sem(f"L{L}_k_mixed_ready{p}") for p in range(2)]

            def sync(self, sp):
                S = self.s

                def spread_q(g):
                    if g.is_number(0):
                        sp.wait_ge(qz_zeroed, 2)
                    sp.wait_ge(S["q_low"], g.count(1, 1))
                    part(sp)
                    wait(sp, S["scores_ps"], g.count(H, -H))
                    for a in range(HG):
                        rows_a = slice(a * DH, (a + 1) * DH)
                        beside = slice((a ^ 1) * DH, ((a ^ 1) + 1) * DH)
                        sp.dma_start(qz[g.par][rows_a, a].bitcast(F32).rearrange("p a t n -> p (a t n)"),
                                     q_parts[rows_a].bitcast(F32).rearrange("p a t n -> p (a t n)")
                                     ).then_inc(self.qz_ready[g.par], 16)
                        sp.dma_start(qz[g.par][beside, a, HIGH].bitcast(F32).rearrange("p t n -> p (t n)"),
                                     q_parts[rows_a, HIGH].bitcast(F32).rearrange("p t n -> p (t n)")
                                     ).then_inc(self.qz_ready[g.par], 16)

                def mix_k(g):
                    sp.wait_ge(S["k_low"], g.count(1, 1))
                    sp.wait_ge(S["k_copied"], g.count(1, 1))
                    for a in range(HG):
                        rows_a = slice(a * DH, (a + 1) * DH)
                        beside = slice((a ^ 1) * DH, ((a ^ 1) + 1) * DH)
                        sp.dma_start(k_mixed[g.par][beside, a % 2].bitcast(F32).rearrange("p t n -> p (t n)"),
                                     k_low_sb[rows_a].bitcast(F32).rearrange("p t n -> p (t n)")
                                     ).then_inc(self.k_mixed_ready[g.par], 16)

                def step(g):
                    if g.is_number(-2):
                        self.load(sp, g + 2)
                        self.load(sp, g + 3)
                    elif g.has(2) and not g.is_number(-1):
                        self.load(sp, g + 2)
                    if g.has(1):
                        spread_q(g + 1)
                        mix_k(g + 1)
                    if g.has(-2):
                        self.store(sp, g + -2)
                return step

            def gpsimd(self, pool):
                S = self.s

                def k_copy(g):
                    pool.wait_ge(S["k_high"], g.count(1, 1))
                    part(pool)
                    nc.gpsimd.tensor_copy(k_mixed[g.par][:, 1].rearrange("p t n -> p (t n)"),
                                          k_mixed[g.par][:, 0].bitcast(F32).rearrange("p t n -> p (t n)")
                                          ).then_inc(S["k_copied"], 1)

                def step(g):
                    if g.has(1):
                        self.pool_residual(pool, g + 1, [bias_o[self.L][:]] * NT)
                        k_copy(g + 1)
                    if g.has(-2):
                        self.pool_rstd(pool, g + -2)
                return step

            def tensor(self, pe):
                S = self.s
                W = {n: wt[(self.L, n)] for n in "qkvo"}

                def project_t(w, bank):
                    for ot in range(DT):
                        last = three_pass(ps[:, bank, ot * N:(ot + 1) * N],
                                          [([w[p][:, kt, ot * P:(ot + 1) * P] for p in (0, 1)],
                                            [xt[p][:, kt, :] for p in (0, 1)]) for kt in range(DT)])
                    return last

                def q(g):
                    pe.wait_ge(S["xt_high"], g.count(1, 1))
                    pe.wait_ge(S["xt_low"], g.count(1, 1))
                    wait(pe, S["v_ready"], g.count())
                    project_t(W["q"], BANK_PROJ).then_inc(S["q_ps"], 1)

                def k(g):
                    wait(pe, S["y_summed"], g.count(1, -2))
                    project_t(W["k"], BANK_PROJ + 1).then_inc(S["k_ps"], 1)

                def v(g, nt):
                    if nt == 0:
                        pe.wait_ge(S["q_low"], g.count(1, 1))
                    last = three_pass(ps[:, BANK_PROJ, nt * D:(nt + 1) * D],
                                      [([xt[p][:, kt, nt * P:(nt + 1) * P] for p in (0, 1)],
                                        [W["v"][p][:, kt, :] for p in (0, 1)]) for kt in range(DT)])
                    if nt == NT - 1:
                        last.then_inc(S["v_ps"], 1)

                def scores(g, h):
                    ot, a = divmod(h, HG)
                    if h == 0:
                        pe.wait_ge(self.qz_ready[g.par], g.turns(32 * HG, 32 * HG))
                        pe.wait_ge(self.k_mixed_ready[g.par], g.turns(16 * HG, 16 * HG))
                    wait(pe, S["max_ready"], g.count(H, h - 1))
                    for qt in range(NT):
                        for i in range(2):
                            last = nc.tensor.matmul(ps[:, BANK_S + h % 2, qt * N:(qt + 1) * N],
                                                    qz[g.par][:, a, i, ot, qt * P:(qt + 1) * P],
                                                    k_mixed[g.par][:, a % 2, ot, :], start=(i == 0), stop=(i == 1))
                    last.then_inc(S["scores_ps"], 1)

                def transpose_probs(g, h):
                    pe.wait_ge(S["exp_ready"], g.count(H, h + 1))
                    wait(pe, S["pt_odd" if h % 2 else "pt_even"], g.count(H // 2, h // 2))
                    for kt in range(NT):
                        for qt in range(NT):
                            last = nc.tensor.transpose(
                                ps[:, BANK_PT + h % 2, kt * N + qt * P:kt * N + (qt + 1) * P],
                                probs[:, h % 4, qt, kt * P:(kt + 1) * P], ident[:])
                    last.then_inc(S["pt_ps"], 1)

                def pv(g, ot):
                    if ot == 0:
                        pe.wait_ge(S["v_ready"], g.count(1, 1))
                        wait(pe, S["o_ready"], g.count())
                    pe.wait_ge(S["pt_even"], g.count(H // 2, 2 * ot + 2))
                    pe.wait_ge(S["pt_odd"], g.count(H // 2, 2 * ot + 2))
                    for kt in range(NT):
                        for a in range(HG):
                            h = ot * HG + a
                            last = nc.tensor.matmul(ps[a * DH:(a + 1) * DH, BANK_O, ot * N:(ot + 1) * N],
                                                    v_sb[:, g.par, kt, h * DH:(h + 1) * DH],
                                                    probs_t[:, h % 4, kt * N:(kt + 1) * N],
                                                    start=(kt == 0), stop=(kt == NT - 1))
                    last.then_inc(S["pv_done"], 1)

                def transpose_recip(g):
                    pe.wait_ge(S["recip_rep_ready"], g.count(1, 1))
                    wait(pe, S["recip_t_ready"], g.count())
                    if g.has(2):
                        pe.wait_ge(S["xt_low"], g.count(1, 3))
                    for ot in range(DT):
                        for qt in range(NT):
                            last = nc.tensor.transpose(
                                ps[:, BANK_X, ot * N + qt * P:ot * N + (qt + 1) * P],
                                recip_rep[:, qt, ot * P:(ot + 1) * P], ident[:])
                    last.then_inc(S["recip_t_ps"], 1)

                def project_out(g):
                    pe.wait_ge(S["o_high"], g.count(1, 1))
                    pe.wait_ge(S["o_low"], g.count(1, 1))
                    wait(pe, S["y_summed"], g.count())
                    if g.has(2):
                        pe.wait_ge(S["k_low"], g.count(1, 3))
                    for nt in range(NT):
                        last = three_pass(ps[:, BANK_PROJ + 1, nt * D:(nt + 1) * D],
                                          [([o_parts[p][:, ot, nt * P:(nt + 1) * P] for p in (0, 1)],
                                            [W["o"][p][:, ot, :] for p in (0, 1)]) for ot in range(DT)])
                    last.then_inc(S["y_ps"], 1)

                def step(g):
                    now, after, before = g.has(0), g.has(1), g.has(-1)
                    for h in range(H):
                        if now:
                            scores(g, h)
                        if h == 3 and before:
                            transpose_recip(g + -1)
                        if h == 6 and g.has(2):
                            wait(pe, S["recip_t_ready"], g.count())
                            self.pe_transpose_x(pe, g + 2)
                        if h == 2 and before:
                            pv(g + -1, 1)
                        if h == 6 and now:
                            pv(g, 0)
                        if h < 2 and before:
                            transpose_probs(g + -1, H - 2 + h)
                        if h >= 2 and now:
                            transpose_probs(g, h - 2)
                        if h == 0 and after:
                            q(g + 1)
                        if h == 1 and after:
                            k(g + 1)
                        if h in (4, 5) and after:
                            v(g + 1, h - 4)
                        if h == 7 and before:
                            project_out(g + -1)
                return step

            def scalar(self, act):
                S = self.s

                def biased(dst, bank, bias, done):
                    for ot in range(DT):
                        last = nc.scalar.activation(dst[:, ot, :], ps[:, bank, ot * N:(ot + 1) * N],
                                                    ACT.Identity, bias=bias[:, ot:ot + 1])
                    last.then_inc(done, 1)

                def q_high(g):
                    act.wait_ge(S["q_ps"], g.count(1, 1))
                    p = g + -1
                    wait(act, self.qz_ready[p.par], p.turns(32 * HG, 32 * HG))
                    biased(q_parts[:, HIGH], BANK_PROJ, bias_q[self.L], S["q_high"])

                def k_high(g):
                    act.wait_ge(S["k_ps"], g.count(1, 1))
                    biased(k_mixed[g.par][:, 0], BANK_PROJ + 1, bias_k[self.L], S["k_high"])

                def v_copy(g):
                    act.wait_ge(S["v_ps"], g.count(1, 1))
                    nc.scalar.activation(v_sb[:, g.par, :, :],
                                         ps[:, BANK_PROJ, :].rearrange("p (t d) -> p t d", t=NT), ACT.Copy
                                         ).then_inc(S["v_ready"], 1)

                def exps(g, h):
                    act.wait_ge(S["max_ready"], g.count(H, h + 1))
                    for qt in range(NT):
                        j = NT * h + qt
                        last = nc.scalar.activation(probs[:, h % 4, qt, :], probs[:, h % 4, qt, :], ACT.Exp,
                                                    bias=neg_max[:, g.par, j:j + 1], scale=-1.0,
                                                    accum_out=sums[:, g.par, j:j + 1])
                    last.then_inc(S["exp_ready"], 1)

                def pt_odd(g, h):
                    act.wait_ge(S["pt_ps"], g.count(H, h + 1))
                    wait(act, S["pv_done"], g.count(2, h // HG))
                    nc.scalar.activation(probs_t[:, h % 4, :], ps[:, BANK_PT + 1, :], ACT.Copy
                                         ).then_inc(S["pt_odd"], 1)

                def recip_t_copy(g):
                    act.wait_ge(S["recip_t_ps"], g.count(1, 1))
                    wait(act, S["o_ready"], g.count())
                    nc.scalar.activation(recip_t[:].rearrange("p t n -> p (t n)"), ps[:, BANK_X, :], ACT.Copy
                                         ).then_inc(S["recip_t_ready"], 1)

                def o_high(g):
                    act.wait_ge(S["o_ready"], g.count(1, 1))
                    wait(act, S["y_ps"], g.count())
                    nc.scalar.activation(o_parts[HIGH][:], o_t[:], ACT.Copy).then_inc(S["o_high"], 1)

                def step(g):
                    now, after, before = g.has(0), g.has(1), g.has(-1)
                    for h in range(H):
                        if h == 0 and before:
                            exps(g + -1, H - 1)
                        if h == 5 and now:
                            pt_odd(g, 3)
                        if h >= 1 and now:
                            exps(g, h - 1)
                        if h == 1 and before:
                            pt_odd(g + -1, H - 1)
                        if h == 6 and g.has(2):
                            self.act_xt_high(act, g + 2, S["v_ps"])
                        if h in (3, 7) and now:
                            pt_odd(g, h - 2)
                        if h == 1 and after:
                            q_high(g + 1)
                        if h == 4 and before:
                            recip_t_copy(g + -1)
                        if h == 5 and before:
                            o_high(g + -1)
                        if h == 2 and after:
                            k_high(g + 1)
                        if h == 5 and after:
                            v_copy(g + 1)
                return step

            def vector(self, dve):
                S = self.s

                def biased_low(low, bank, bias, high, done):
                    for ot in range(DT):
                        last = nc.vector.scalar_tensor_tensor(
                            out=low[:, ot, :], in0=ps[:, bank, ot * N:(ot + 1) * N],
                            scalar=bias[:, ot:ot + 1], in1=high[:, ot, :].bitcast(F32),
                            op0=ALU.add, op1=ALU.subtract)
                    last.then_inc(done, 1)

                def q_low(g):
                    dve.wait_ge(S["q_high"], g.count(1, 1))
                    biased_low(q_parts[:, LOW], BANK_PROJ, bias_q[self.L], q_parts[:, HIGH], S["q_low"])

                def k_low(g):
                    dve.wait_ge(S["k_high"], g.count(1, 1))
                    p = g + -1
                    wait(dve, self.k_mixed_ready[p.par], p.turns(16 * HG, 16 * HG))
                    biased_low(k_low_sb, BANK_PROJ + 1, bias_k[self.L], k_mixed[g.par][:, 0], S["k_low"])

                def masked_max(g, h):
                    dve.wait_ge(S["scores_ps"], g.count(H, h + 1))
                    wait(dve, S["pt_ps"], g.count(H, h - 3))
                    part(dve)
                    for qt in range(NT):
                        j = NT * h + qt
                        last = nc.vector.tensor_tensor_reduce(
                            probs[:, h % 4, qt, :], ps[:, BANK_S + h % 2, qt * N:(qt + 1) * N],
                            mask[:, qt, :], -SCALE, HIGHEST, ALU.add, ALU.min, neg_max[:, g.par, j:j + 1])
                    last.then_inc(S["max_ready"], 1)

                def pt_even(g, h):
                    dve.wait_ge(S["pt_ps"], g.count(H, h + 1))
                    wait(dve, S["pv_done"], g.count(2, h // HG))
                    nc.vector.tensor_copy(probs_t[:, h % 4, :], ps[:, BANK_PT, :]).then_inc(S["pt_even"], 1)

                def recip_sums(g):
                    dve.wait_ge(S["exp_ready"], g.count(H, H))
                    nc.vector.reciprocal(recip[:], sums[:, g.par, :]).then_inc(S["recip_ready"], 1)
                    dve.wait_ge(S["recip_ready"], g.count(1, 1))
                    wait(dve, S["recip_t_ps"], g.count())
                    r = recip[:].rearrange("p (h q) -> p h q", q=NT)
                    for qt in range(NT):
                        last = nc.vector.tensor_scalar(recip_rep[:, qt].rearrange("p (h d) -> p h d", h=H),
                                                       r[:, :, qt:qt + 1].to_broadcast([P, H, DH]),
                                                       defined[:, qt:qt + 1], None, ALU.mult)
                    last.then_inc(S["recip_rep_ready"], 1)

                def normalize_o(g):
                    dve.wait_ge(S["pv_done"], g.count(2, 2))
                    dve.wait_ge(S["recip_t_ready"], g.count(1, 1))
                    wait(dve, S["o_low"], g.count())
                    nc.vector.tensor_tensor(o_t[:].rearrange("p t n -> p (t n)"), ps[:, BANK_O, :],
                                            recip_t[:].rearrange("p t n -> p (t n)"), ALU.mult
                                            ).then_inc(S["o_ready"], 1)

                def o_low(g):
                    dve.wait_ge(S["o_high"], g.count(1, 1))
                    nc.vector.tensor_tensor(o_parts[LOW][:].rearrange("p t n -> p (t n)"),
                                            o_t[:].rearrange("p t n -> p (t n)"),
                                            o_parts[HIGH][:].bitcast(F32).rearrange("p t n -> p (t n)"),
                                            ALU.subtract).then_inc(S["o_low"], 1)

                def y_sum(g):
                    dve.wait_ge(S["y_ps"], g.count(1, 1))
                    dve.wait_ge(S["residual_ready"], g.count(1, 1))
                    wait(dve, S["out_ready"], g.count())
                    nc.vector.tensor_tensor(y_sb[:].rearrange("p t d -> p (t d)"), ps[:, BANK_PROJ + 1, :],
                                            self.x_of(g), ALU.add).then_inc(S["y_summed"], 1)

                def step(g):
                    now, after, before = g.has(0), g.has(1), g.has(-1)
                    for h in range(H):
                        if now:
                            masked_max(g, h)
                        if h == 0 and before:
                            pt_even(g + -1, H - 2)
                        if h in (2, 4, 6) and now:
                            pt_even(g, h - 2)
                        if h == 0 and g.has(-2):
                            y_sum(g + -2)
                        if h == 1 and before:
                            recip_sums(g + -1)
                        if h == 1 and after:
                            q_low(g + 1)
                        if h == 3 and after:
                            k_low(g + 1)
                        if h == 3 and g.has(-2):
                            self.dve_stats(dve, g + -2)
                        if h == 4 and before:
                            normalize_o(g + -1)
                        if h == 5 and before:
                            o_low(g + -1)
                        if h == 6 and g.has(2):
                            self.dve_xt_low(dve, g + 2)
                        if h == 7 and g.has(-2):
                            self.dve_normalize(dve, g + -2)
                return step

        class GraphAttention(Layer):

            def __init__(self, L):
                super().__init__(L, ["dst_ps", "max_ready", "wh_ps", "e_src_ready", "wh_ready", "src_max",
                                     "row_max", "neg_max_ready", "summed", "logits_ready", "exp_ready",
                                     "pt_ps", "pt_ready", "recip_raw", "recip_ready",
                                     "neg_mean_ready", "shift_ready"])

            def sync(self, sp):
                def step(g):
                    if g.has(2):
                        self.load(sp, g + 2)
                    if g.has(-4):
                        self.store(sp, g + -4)
                return step

            def gpsimd(self, pool):
                def step(g):
                    if g.has(-2):
                        self.pool_rstd(pool, g + -2)
                        self.pool_shift(pool, g + -2)
                return step

            def tensor(self, pe):
                S = self.s

                def dst_rows(g):
                    pe.wait_ge(S["xt_high"], g.count(1, 1))
                    pe.wait_ge(S["xt_low"], g.count(1, 1))
                    wait(pe, S["max_ready"], g.count())
                    three_pass(ps[:, 1, 0:N],
                               [([dst_rep[p][:, kt, :] for p in (0, 1)], [self.xt(g)[p][:, kt, :] for p in (0, 1)])
                                for kt in range(DT)]).then_inc(S["dst_ps"], 1)

                def wh(g):
                    if g.is_number(0):
                        pe.wait_ge(layers[1].s["y_summed"], B)
                    wait(pe, S["wh_ready"], g.count())
                    for nt in range(NT):
                        last = three_pass(ps[:, 2 + nt, 0:WE],
                                          [([self.xt(g)[p][:, kt, nt * P:(nt + 1) * P] for p in (0, 1)],
                                            [w2[p][:, kt, :] for p in (0, 1)]) for kt in range(DT)])
                    last.then_inc(S["wh_ps"], 1)

                def transpose_probs(g):
                    pe.wait_ge(S["exp_ready"], g.count(1, 1))
                    wait(pe, S["pt_ready"], g.count())
                    for mt in range(NT):
                        for nt in range(NT):
                            last = nc.tensor.transpose(ps[:, 4, mt * N + nt * P:mt * N + (nt + 1) * P],
                                                       probs[:, 2 + g.par, nt, mt * P:(mt + 1) * P], ident[:])
                    last.then_inc(S["pt_ps"], 1)

                def weighted_sum(g):
                    pe.wait_ge(S["pt_ready"], g.count(1, 1))
                    pe.wait_ge(S["wh_ready"], g.count(1, 1))
                    wait(pe, S["y_summed"], g.count(1, -1))
                    for nt in range(NT):
                        for mt in range(NT):
                            last = nc.tensor.matmul(ps[:, 6 + g.par, nt * D:(nt + 1) * D],
                                                    probs_t[:, 0, mt * N + nt * P:mt * N + (nt + 1) * P],
                                                    v_sb[:, g.par, mt, :], start=(mt == 0), stop=(mt == NT - 1))
                    last.then_inc(S["y_ps"], 1)

                def step(g):
                    if g.has(-1):
                        transpose_probs(g + -1)
                    if g.has(2):
                        self.pe_transpose_x(pe, g + 2)
                    if g.has(1):
                        dst_rows(g + 1)
                        wh(g + 1)
                    if g.has(-1):
                        weighted_sum(g + -1)
                return step

            def scalar(self, act):
                S = self.s

                def wh_copy(g):
                    act.wait_ge(S["wh_ps"], g.count(1, 1))
                    wait(act, S["y_ps"], g.count(1, -1))
                    nc.scalar.activation(v_sb[:, g.par, :, :], ps[:, 2:4, 0:D], ACT.Copy
                                         ).then_inc(S["wh_ready"], 1)

                def e_src_copy(g):
                    act.wait_ge(S["wh_ps"], g.count(1, 1))
                    wait(act, S["src_max"], g.count(1, -1))
                    nc.scalar.activation(e_src[:, g.par, :], ps[:, 2:4, D], ACT.Copy
                                         ).then_inc(S["e_src_ready"], 1)

                def source_sum(g):
                    act.wait_ge(S["e_src_ready"], g.count(1, 1))
                    act.wait_ge(S["max_ready"], g.count(1, 1))
                    wait(act, S["logits_ready"], g.count())
                    for nt in range(NT):
                        last = nc.scalar.activation(probs[:, 1, nt, :], probs[:, 0, nt, :], ACT.Identity,
                                                    bias=e_src[:, g.par, nt:nt + 1])
                    last.then_inc(S["summed"], 1)

                def exps(g):
                    act.wait_ge(S["logits_ready"], g.count(1, 1))
                    act.wait_ge(S["neg_max_ready"], g.count(1, 1))
                    wait(act, S["recip_raw"], g.count(1, -1))
                    for nt in range(NT):
                        last = nc.scalar.activation(probs[:, 2 + g.par, nt, :], probs[:, 2 + g.par, nt, :],
                                                    ACT.Exp, bias=node_max[:, 2, nt:nt + 1],
                                                    accum_out=sums[:, g.par, nt:nt + 1])
                    last.then_inc(S["exp_ready"], 1)

                def step(g):
                    if g.has(0):
                        wh_copy(g)
                    if g.has(2):
                        self.act_xt_high(act, g + 2, S["wh_ps"])
                    if g.has(0):
                        exps(g)
                    if g.has(-3):
                        self.act_normalize(act, g + -3)
                    if g.has(1):
                        e_src_copy(g + 1)
                        source_sum(g + 1)
                return step

            def vector(self, dve):
                S = self.s

                def masked_max(g):
                    dve.wait_ge(S["dst_ps"], g.count(1, 1))
                    wait(dve, S["summed"], g.count())
                    part(dve)
                    for nt in range(NT):
                        last = nc.vector.tensor_tensor_reduce(probs[:, 0, nt, :], ps[:, 1, 0:N], mask[:, nt, :],
                                                              1.0, LOWEST, ALU.add, ALU.max,
                                                              maxes[:, g.par, nt:nt + 1])
                    last.then_inc(S["max_ready"], 1)

                def pt_copy(g):
                    dve.wait_ge(S["pt_ps"], g.count(1, 1))
                    wait(dve, S["y_ps"], g.count())
                    nc.vector.tensor_scalar(probs_t[:, 0, :], ps[:, 4, :], 0.0, None, ALU.max
                                            ).then_inc(S["pt_ready"], 1)

                def raw_recip(g):
                    dve.wait_ge(S["exp_ready"], g.count(1, 1))
                    nc.vector.reciprocal(src_recip[:, 0, :], sums[:, g.par, :NT]).then_inc(S["recip_raw"], 1)

                def guarded_recip(g):
                    dve.wait_ge(S["recip_raw"], g.count(1, 1))
                    nc.vector.scalar_tensor_tensor(out=src_recip[:, 1, :], in0=src_recip[:, 0, :], scalar=0.0,
                                                   in1=row_any[:], op0=ALU.max, op1=ALU.mult
                                                   ).then_inc(S["recip_ready"], 1)

                def source_max(g):
                    dve.wait_ge(S["e_src_ready"], g.count(1, 1))
                    dve.wait_ge(S["max_ready"], g.count(1, 1))
                    nc.vector.tensor_tensor(node_max[:, 0, :], maxes[:, g.par, 0:NT], e_src[:, g.par, :], ALU.add
                                            ).then_inc(S["src_max"], 1)

                def row_max(g):
                    dve.wait_ge(S["src_max"], g.count(1, 1))
                    nc.vector.scalar_tensor_tensor(out=node_max[:, 1, :], in0=node_max[:, 0, :], scalar=NEG_SLOPE,
                                                   in1=node_max[:, 0, :], op0=ALU.mult, op1=ALU.max
                                                   ).then_inc(S["row_max"], 1)

                def negated_max(g):
                    dve.wait_ge(S["row_max"], g.count(1, 1))
                    wait(dve, S["exp_ready"], g.count())
                    nc.vector.tensor_scalar(node_max[:, 2, :], node_max[:, 1, :], -1.0, None, ALU.mult
                                            ).then_inc(S["neg_max_ready"], 1)

                def leaky(g):
                    dve.wait_ge(S["summed"], g.count(1, 1))
                    wait(dve, S["pt_ps"], g.count(1, -1))
                    nc.vector.scalar_tensor_tensor(out=probs[:, 2 + g.par].rearrange("p t n -> p (t n)"),
                                                   in0=probs[:, 1].rearrange("p t n -> p (t n)"),
                                                   scalar=NEG_SLOPE,
                                                   in1=probs[:, 1].rearrange("p t n -> p (t n)"),
                                                   op0=ALU.mult, op1=ALU.max).then_inc(S["logits_ready"], 1)

                def y_sum(g):
                    dve.wait_ge(S["y_ps"], g.count(1, 1))
                    dve.wait_ge(S["recip_ready"], g.count(1, 1))
                    wait(dve, S["out_ready"], g.count(1, -1))
                    for nt in range(NT):
                        last = nc.vector.scalar_tensor_tensor(
                            out=self.y(g)[:, nt, :], in0=ps[:, 6 + g.par, nt * D:(nt + 1) * D],
                            scalar=src_recip[:, 1, nt:nt + 1], in1=self.x_of(g, slice(nt, nt + 1)),
                            op0=ALU.mult, op1=ALU.add)
                    last.then_inc(S["y_summed"], 1)

                def step(g):
                    if g.has(0):
                        source_max(g)
                    if g.has(-2):
                        y_sum(g + -2)
                    if g.has(0):
                        row_max(g)
                        leaky(g)
                        negated_max(g)
                    if g.has(-1):
                        pt_copy(g + -1)
                        raw_recip(g + -1)
                    if g.has(2):
                        self.dve_xt_low(dve, g + 2)
                    if g.has(1):
                        masked_max(g + 1)
                    if g.has(-1):
                        guarded_recip(g + -1)
                    if g.has(-2):
                        self.dve_stats(dve, g + -2)
                return step

        layers = [MessagePassing(0), Attention(1), GraphAttention(2), Attention(3)]

        def opening(eng, L):
            before = layers[L - 1]
            if eng is nc.sync:
                for p in range(2):
                    eng.wait_ge(layer_done[L - 1][p], 16)
                eng.wait_ge(before.s["xt_ps"], B)
                if L - 1 != 2:
                    eng.wait_ge(before.s["residual_ready"], B)
            if eng is nc.tensor:
                eng.wait_ge(before.s["xt_low"], B)
                for name in {0: ["mi_scaled"], 1: ["recip_t_ready", "o_ready", "v_ready"],
                             2: ["wh_ready", "e_src_ready"]}[L - 1]:
                    eng.wait_ge(before.s[name], B)

        block = ctx.enter_context(nc.Block())

        @block.sync
        def _(sp):
            prep_sync(sp)
            run_layers(sp, [layer.sync(sp) for layer in layers], opening, start_of_layer, TRANSFERS_OPENED_AFTER)
            sp.wait_ge(layer_done[3][0], 16 * (B // 2))
            sp.wait_ge(layer_done[3][1], 16 * (B // 2))

        @block.gpsimd
        def _(pool):
            prep_gpsimd(pool)
            run_layers(pool, [layer.gpsimd(pool) for layer in layers], opening, start_of_layer, OPENED_AFTER)

        @block.tensor
        def _(pe):
            prep_tensor(pe)
            run_layers(pe, [layer.tensor(pe) for layer in layers], opening, start_of_layer, OPENED_AFTER)

        @block.scalar
        def _(act):
            prep_scalar(act)
            run_layers(act, [layer.scalar(act) for layer in layers], opening, start_of_layer, OPENED_AFTER)

        @block.vector
        def _(dve):
            prep_vector(dve)
            run_layers(dve, [layer.vector(dve) for layer in layers], opening, start_of_layer, OPENED_AFTER)


_INS = ["x", "adj", "L0_gnn_W", "L0_gnn_b", "L1_gnn_Wq", "L1_gnn_bq", "L1_gnn_Wk", "L1_gnn_bk", "L1_gnn_Wv",
        "L1_gnn_bv", "L1_gnn_Wo", "L1_gnn_bo", "L2_gnn_W", "L2_gnn_a_src", "L2_gnn_a_dst", "L3_gnn_Wq",
        "L3_gnn_bq", "L3_gnn_Wk", "L3_gnn_bk", "L3_gnn_Wv", "L3_gnn_bv", "L3_gnn_Wo", "L3_gnn_bo"]


def kernel(**inputs):
    import numpy as _np
    import concourse.bacc as _bacc
    from concourse import mybir as _mybir
    from concourse.bass_utils import run_bass_kernel_spmd as _run

    nc = _bacc.Bacc("TRN2", target_bir_lowering=False, num_devices=1)
    arrays, args = {}, []
    for name in _INS:
        a = _np.ascontiguousarray(inputs[name])
        arrays[f"in_{name}"] = a
        args.append(nc.dram_tensor(f"in_{name}", a.shape, _mybir.dt.from_np(a.dtype), kind="ExternalInput").ap())
    args.append(nc.dram_tensor("out_y", (B, N, D), _mybir.dt.float32, kind="ExternalOutput").ap())
    graph_layers_kernel(nc, *args)
    r = _run(nc, [arrays], core_ids=[0])
    return r.results[0]["out_y"]
```
